# Optimizing a Trainium2 kernel written in Bass

```python
import numpy as np
import jax
import jax.numpy as jnp

def _softmax(x, axis=-1):
    return jax.nn.softmax(x, axis=axis)

def _gelu(x):
    return jax.nn.gelu(x, approximate=True)

def _silu(x):
    return jax.nn.silu(x)

def _sigmoid(x):
    return jax.nn.sigmoid(x)

def _layernorm(x, axis=-1, eps=1e-05):
    m = jnp.mean(x, axis=axis, keepdims=True)
    v = jnp.var(x, axis=axis, keepdims=True)
    return (x - m) / jnp.sqrt(v + eps)

def _scatter_add(tgt, idx, src, axis=0):
    return tgt.at[idx].add(src)

def _segment_sum(src, seg, n):
    return jax.ops.segment_sum(src, seg, n)
kernel_name = 'mk_adaln_ffn_d2_seqx_r4_b0289d'

def setup_inputs(seed: int=0):
    np.random.seed(seed)
    _w = jnp.asarray

    def _rec_inputs():
        import jax
        import jax.numpy as jnp
        _rk = jax.random.key(seed)
        x = -0.000125 + 0.9999 * jax.random.normal(jax.random.fold_in(_rk, 1), (2, 1024, 256), jnp.float32)
        _lenS = 1024 - jax.random.randint(jax.random.fold_in(_rk, 7), (2,), 0, max(1, 1024 // 4) + 1, jnp.int32)
        _lenS2 = 1024 - jax.random.randint(jax.random.fold_in(_rk, 8), (2,), 0, max(1, 1024 // 4) + 1, jnp.int32)
        cond_1024 = 0.00513981 + 1.0024 * jax.random.normal(jax.random.fold_in(_rk, 11), (2, 256), jnp.float32)
        return (x, cond_1024)
    x, cond_1024 = _rec_inputs()

    def _L0_cond_setup():
        import jax, jax.numpy as jnp
        import numpy as np
        IN_FEATURES = 256
        OUT_FEATURES = 256
        BATCH = 32
        SEQ = 256
        EPS = 1e-08
        key = jax.random.key(seed)
        k1, k2, k3 = jax.random.split(key, 3)
        Efou = jax.random.normal(k1, (BATCH, SEQ, IN_FEATURES), dtype=jnp.float32)
        y = jax.random.normal(k2, (BATCH, IN_FEATURES), dtype=jnp.float32)
        weight = jax.random.normal(k3, (IN_FEATURES, OUT_FEATURES), dtype=jnp.float32)
        return {'Efou': Efou, 'y': y, 'weight': weight}
    _L0_cond_all = _L0_cond_setup()
    _L0_cond_in = {k: v for k, v in _L0_cond_all.items() if k in ('weight',)}
    del _L0_cond_all

    def _L0_ffn_setup():
        import jax, jax.numpy as jnp
        import numpy as np
        BLOCK = 16
        _GRID = jnp.array([0.0, 0.5, 1.0, 1.5, 2.0, 3.0, 4.0, 6.0], dtype=jnp.float32)
        _MID = jnp.array([0.25, 0.75, 1.25, 1.75, 2.5, 3.5, 5.0], dtype=jnp.float32)

        def fp4_quant_dequant(x):
            shape = x.shape
            xb = x.reshape(shape[:-1] + (shape[-1] // BLOCK, BLOCK))
            scale = jnp.max(jnp.abs(xb), axis=-1, keepdims=True) / 6.0
            scale = jnp.maximum(scale, jnp.float32(1e-12))
            xn = xb / scale
            idx = jnp.searchsorted(_MID, jnp.abs(xn))
            q = _GRID[idx] * jnp.sign(xn) * scale
            return q.reshape(shape)

        def fp4_linear(x, w):
            xq = fp4_quant_dequant(x)
            wq = fp4_quant_dequant(w)
            return jnp.einsum('bsk,nk->bsn', xq, wq)
        key = jax.random.key(seed)
        k1, k2, k3, k4 = jax.random.split(key, 4)
        H, I = (256, 704)
        x = jax.random.normal(k1, (4, 1024, H), dtype=jnp.float32)
        w_gate = jax.random.normal(k2, (I, H), dtype=jnp.float32) * 0.02
        w_up = jax.random.normal(k3, (I, H), dtype=jnp.float32) * 0.02
        w_down = jax.random.normal(k4, (H, I), dtype=jnp.float32) * 0.02
        return {'x': x, 'w_gate': w_gate, 'w_up': w_up, 'w_down': w_down}
    _L0_ffn_all = _L0_ffn_setup()
    _L0_ffn_in = {k: v for k, v in _L0_ffn_all.items() if k in ('w_gate', 'w_up', 'w_down')}
    del _L0_ffn_all

    def _L1_cond_setup():
        import jax, jax.numpy as jnp
        import numpy as np
        B, L, D_IN, D = (64, 128, 256, 256)
        key = jax.random.key(seed)
        k1, k2, k3, k4, k5 = jax.random.split(key, 5)
        x = jax.random.normal(k1, (B, L, D_IN), dtype=jnp.float32)
        Wk = jax.random.normal(k2, (D_IN, 3 * D), dtype=jnp.float32) * (1.0 / np.sqrt(D_IN))
        Wr = jax.random.normal(k3, (D, 3 * D), dtype=jnp.float32) * (1.0 / np.sqrt(D))
        c0 = jax.random.normal(k4, (B, D), dtype=jnp.float32)
        h0 = jax.random.normal(k5, (B, D), dtype=jnp.float32)
        return {'x': x, 'Wk': Wk, 'Wr': Wr, 'c0': c0, 'h0': h0}
    _L1_cond_all = _L1_cond_setup()
    _L1_cond_in = {k: v for k, v in _L1_cond_all.items() if k in ('Wk', 'Wr')}
    del _L1_cond_all

    def _L1_ffn_setup():
        import jax, jax.numpy as jnp
        import numpy as np
        B, K, D = (128, 32, 256)
        E = 32
        H = int(D * 0.25)

        def _rsqrt_uniform(key, shape, d):
            bound = d ** (-0.5)
            return jax.random.uniform(key, shape, jnp.float32, -bound, bound)
        key = jax.random.key(seed)
        ks = jax.random.split(key, 7)
        return {'x': jax.random.normal(ks[0], (B, K, D), jnp.float32), 'router_w': _rsqrt_uniform(ks[1], (E, D), D), 'router_b': _rsqrt_uniform(ks[2], (E,), D), 'weights1': _rsqrt_uniform(ks[3], (E, D, H), H), 'bias1': _rsqrt_uniform(ks[4], (E, H), H), 'weights2': _rsqrt_uniform(ks[5], (E, H, D), D), 'bias2': _rsqrt_uniform(ks[6], (E, D), D)}
    _L1_ffn_all = _L1_ffn_setup()
    _L1_ffn_in = {k: v for k, v in _L1_ffn_all.items() if k in ('router_w', 'router_b', 'weights1', 'bias1', 'weights2', 'bias2')}
    del _L1_ffn_all
    return {'x': x, 'cond_1024': cond_1024, 'L0_cond_weight': _L0_cond_in['weight'], 'L0_ffn_w_gate': _L0_ffn_in['w_gate'], 'L0_ffn_w_up': _L0_ffn_in['w_up'], 'L0_ffn_w_down': _L0_ffn_in['w_down'], 'L1_cond_Wk': _L1_cond_in['Wk'], 'L1_cond_Wr': _L1_cond_in['Wr'], 'L1_ffn_router_w': _L1_ffn_in['router_w'], 'L1_ffn_router_b': _L1_ffn_in['router_b'], 'L1_ffn_weights1': _L1_ffn_in['weights1'], 'L1_ffn_bias1': _L1_ffn_in['bias1'], 'L1_ffn_weights2': _L1_ffn_in['weights2'], 'L1_ffn_bias2': _L1_ffn_in['bias2']}

def reference(x, cond_1024, L0_cond_weight, L0_ffn_w_gate, L0_ffn_w_up, L0_ffn_w_down, L1_cond_Wk, L1_cond_Wr, L1_ffn_router_w, L1_ffn_router_b, L1_ffn_weights1, L1_ffn_bias1, L1_ffn_weights2, L1_ffn_bias2):
    import jax
    import jax.numpy as jnp

    def _L0_cond_ref(Efou, y, weight):
        import jax, jax.numpy as jnp
        import numpy as np
        IN_FEATURES = 256
        OUT_FEATURES = 256
        BATCH = 32
        SEQ = 256
        EPS = 1e-08
        scale = 1.0 / np.sqrt(np.float32(weight.shape[0]))
        ys = y * scale
        d = jax.lax.rsqrt(jnp.einsum('bi,io->bo', ys * ys, weight * weight) + EPS)
        out = jnp.einsum('bsi,io->bso', Efou * ys[:, None, :], weight) * d[:, None, :]
        return out

    def _L0_ffn_ref(x, w_gate, w_up, w_down):
        import jax, jax.numpy as jnp
        import numpy as np
        BLOCK = 16
        _GRID = jnp.array([0.0, 0.5, 1.0, 1.5, 2.0, 3.0, 4.0, 6.0], dtype=jnp.float32)
        _MID = jnp.array([0.25, 0.75, 1.25, 1.75, 2.5, 3.5, 5.0], dtype=jnp.float32)

        def fp4_quant_dequant(x):
            shape = x.shape
            xb = x.reshape(shape[:-1] + (shape[-1] // BLOCK, BLOCK))
            scale = jnp.max(jnp.abs(xb), axis=-1, keepdims=True) / 6.0
            scale = jnp.maximum(scale, jnp.float32(1e-12))
            xn = xb / scale
            idx = jnp.searchsorted(_MID, jnp.abs(xn))
            q = _GRID[idx] * jnp.sign(xn) * scale
            return q.reshape(shape)

        def fp4_linear(x, w):
            xq = fp4_quant_dequant(x)
            wq = fp4_quant_dequant(w)
            return jnp.einsum('bsk,nk->bsn', xq, wq)
        gate = fp4_linear(x, w_gate)
        y = fp4_linear(x, w_up)
        h = jax.nn.silu(gate) * y
        return fp4_linear(h, w_down)

    def _L1_cond_ref(x, Wk, Wr, c0, h0):
        import jax, jax.numpy as jnp
        import numpy as np
        B, L, D_IN, D = (64, 128, 256, 256)
        x_proj = jnp.einsum('bli,ig->blg', x, Wk)

        def step(carry, xp_t):
            c, h = carry
            gates = xp_t + h @ Wr
            f, o, g = jnp.split(gates, 3, axis=-1)
            sf = jax.nn.sigmoid(f)
            c_new = c * sf + (1.0 - sf) * jnp.tanh(g)
            h_new = jax.nn.sigmoid(o) * jnp.tanh(c_new)
            return ((c_new, h_new), h_new)
        _, hs = jax.lax.scan(step, (c0, h0), jnp.swapaxes(x_proj, 0, 1))
        return jnp.swapaxes(hs, 0, 1)

    def _L1_ffn_ref(x, router_w, router_b, weights1, bias1, weights2, bias2):
        import jax, jax.numpy as jnp
        import numpy as np
        B, K, D = (128, 32, 256)
        E = 32
        H = int(D * 0.25)

        def _rsqrt_uniform(key, shape, d):
            bound = d ** (-0.5)
            return jax.random.uniform(key, shape, jnp.float32, -bound, bound)
        b, k, d = x.shape
        x_flat = x.reshape(-1, d)
        n = x_flat.shape[0]
        logits = x_flat @ router_w.T + router_b
        routed_idx = jnp.argmax(logits, axis=-1)

        def expert_mlp(w1, b1, w2, b2):
            h = jax.nn.relu(x_flat @ w1 + b1)
            return jax.nn.relu(h @ w2 + b2)
        y_all = jax.vmap(expert_mlp)(weights1, bias1, weights2, bias2)
        out_flat = y_all[routed_idx, jnp.arange(n)]
        return out_flat.reshape(b, k, d)
    x = x + _L0_ffn_ref(_L0_cond_ref(x, cond_1024, L0_cond_weight), L0_ffn_w_gate, L0_ffn_w_up, L0_ffn_w_down)
    x = x + _L1_ffn_ref(_L1_cond_ref(x, L1_cond_Wk, L1_cond_Wr, cond_1024, cond_1024), L1_ffn_router_w, L1_ffn_router_b, L1_ffn_weights1, L1_ffn_bias1, L1_ffn_weights2, L1_ffn_bias2)
    return x

_drawn_inputs = setup_inputs


def setup_inputs(seed=0):
    import zlib

    import numpy as np

    out = dict(_drawn_inputs(seed))
    spreads = {}
    factors = {'L1_ffn_bias1': 6.042}
    for name, (base, spread) in spreads.items():
        noise = np.random.default_rng([zlib.crc32(name.encode()), seed]).standard_normal(out[name].shape)
        drawn = base * np.exp(spread * noise) if base else spread * noise
        out[name] = jnp.asarray(drawn.astype(out[name].dtype))
    for name, factor in factors.items():
        out[name] = (out[name] * factor).astype(out[name].dtype)
    return out
```

```python
from contextlib import ExitStack

import concourse.bass as bass
from concourse import mybir

ALU = mybir.AluOpType
ACT = mybir.ActivationFunctionType
AX = mybir.AxisListType
F32 = mybir.dt.float32
F16 = mybir.dt.float16
BF16 = mybir.dt.bfloat16
I32 = mybir.dt.int32

P = 128
QB = 16
W_SCALE = 32.0
H_SCALE = 16.0
GATE_SCALE = W_SCALE * H_SCALE


def build(nc, x, xt, condt, w_mod, w_gu, w_down, wk, wr, router, router_b, w1, b1, w2, b2, out):
    CH, _, KD, _ = xt.shape
    B = condt.shape[2]
    D = KD * P
    STEPS = P // B
    GU = w_gu.shape[1]
    FF = GU * 64
    KF = (FF + P - 1) // P
    FR = FF - (KF - 1) * P
    G3 = wk.shape[2]
    E = router.shape[2]
    HID = w1.shape[2]
    NB = HID // P
    GRP = 4
    WQ = GU * D + KD * FF

    with ExitStack() as ctx:
        def sb(name, shape, dt=F32):
            return ctx.enter_context(nc.sbuf_tensor(name, shape, dt))

        def bank(name):
            return ctx.enter_context(nc.psum_tensor(name, [P, 512], F32))

        def sem(name):
            return ctx.enter_context(nc.semaphore(name))

        gate_g, gate_f, gate_o = bank("gate_g"), bank("gate_f"), bank("gate_o")
        turn_a, turn_b = bank("turn_a"), bank("turn_b")
        mm_a, mm_b, mm_c = bank("mm_a"), bank("mm_b"), bank("mm_c")

        wq_in = sb("wq_in", [P, WQ])
        wq_v = sb("wq_v", [P, WQ])
        wq_t = sb("wq_t", [P, WQ])
        wq_c = sb("wq_c", [P, WQ])
        wgu_t = sb("wgu_t", [P, KD, GU * P])
        wdown_t = sb("wdown_t", [P, KF, D])
        wmod = sb("wmod", [P, KD, D])
        wmod2 = sb("wmod2", [P, KD, D])
        wk_s = sb("wk_s", [P, KD, G3])
        wr_s = sb("wr_s", [P, KD, G3])
        wr_hi = sb("wr_hi", [P, KD, G3], F16)
        wr_lo = sb("wr_lo", [P, KD, G3], F16)
        router_s = sb("router_s", [P, KD, E])
        rb_s = sb("rb_s", [1, E])
        w1_s = sb("w1_s", [P, KD, HID])
        b1_s = sb("b1_s", [P, NB])
        w2_s = sb("w2_s", [P, NB, D])
        b2_s = sb("b2_s", [E, D])
        ident = sb("ident", [P, P])
        ones = sb("ones", [P, P])
        zeros = sb("zeros", [P, 512], F16)
        spread = sb("spread", [E, HID], BF16)
        spread_a = sb("spread_a", [E, HID], BF16)
        iota_m = sb("iota_m", [P, E])
        cond_s = sb("cond_s", [P, KD, B])
        ys = sb("ys", [P, KD, B])
        ys2 = sb("ys2", [P, KD, B])
        ys2_b = sb("ys2_b", [P, KD, B, STEPS])
        dvar = sb("dvar", [P, D])
        dsq = sb("dsq", [P, D])
        dinv = sb("dinv", [P, D])
        dtmp = sb("dtmp", [P, D])
        demod = sb("demod", [P, D])
        x_s = sb("x_s", [P, D])
        xt_s = sb("xt_s", [P, KD, P])
        xm = sb("xm", [P, KD, P])
        o_s = sb("o_s", [P, D])
        oq = sb("oq", [P, D])
        oq_t = sb("oq_t", [P, KD, P])
        sig = sb("sig", [P, FF])
        gs = sb("gs", [P, FF])
        hh = sb("hh", [P, FF])
        hq = sb("hq", [P, FF])
        hq_t = sb("hq_t", [P, KF, P])
        q_amax = sb("q_amax", [P, WQ // QB])
        q_inv = sb("q_inv", [P, WQ // QB])
        q_scale = sb("q_scale", [P, WQ // QB])
        q_v = sb("q_v", [P, FF])
        q_c = sb("q_c", [P, FF])
        q_t = sb("q_t", [P, FF])
        x1 = sb("x1", [P, D])
        x1_t = sb("x1_t", [P, KD, P])
        h16 = sb("h16", [P, 2, 2, KD, B], F16)
        fold0 = sb("fold0", [P, 2, 4 * KD * B + 4])
        fold1 = sb("fold1", [P, 4 * KD * B + 4])
        so = sb("so", [P, KD * B])
        tc = sb("tc", [P, KD * B])
        hist = sb("hist", [P, STEPS, KD, B])
        ht = sb("ht", [P, KD, P])
        top = sb("top", [P, 1])
        cand = sb("cand", [P, E])
        first = sb("first", [P, 1])
        onehot = sb("onehot", [P, E])
        oh_t = sb("oh_t", [E, P])
        oh_tb = sb("oh_tb", [E, P], BF16)
        hid = sb("hid", [P, 2, GRP, P])
        hidm = sb("hidm", [P, 2, GRP, P])
        y_s = sb("y_s", [P, D])

        in_wq, in_mod, in_rec, in_moe = sem("in_wq"), sem("in_mod"), sem("in_rec"), sem("in_moe")
        in_x = sem("in_x")
        consts = sem("consts")
        setup_v = sem("setup_v")
        setup_pe = sem("setup_pe")
        setup_act = sem("setup_act")
        wq_turned, wq_kept = sem("wq_turned"), sem("wq_kept")
        chain = sem("chain")
        xm_ready, mod_done = sem("xm_ready"), sem("mod_done")
        oq_ready, oq_turned, oqt_ready = sem("oq_ready"), sem("oq_turned"), sem("oqt_ready")
        gu_done, sig_ready = sem("gu_done"), sem("sig_ready")
        hq_ready, hq_turned, hqt_ready = sem("hq_ready"), sem("hq_turned"), sem("hqt_ready")
        down_done, x1_ready, x1_turned, x1t_ready = (sem("down_done"), sem("x1_ready"),
                                                    sem("x1_turned"), sem("x1t_ready"))
        xp_done, xp_ready = sem("xp_done"), sem("xp_ready")
        g_done, f_done, o_done = sem("g_done"), sem("f_done"), sem("o_done")
        f_ready, tc_ready = sem("f_ready"), sem("tc_ready")
        c_ready, hi_ready, h_ready, lo_ready = sem("c_ready"), sem("hi_ready"), sem("h_ready"), sem("lo_ready")
        ht_ready, logits_done, top_ready = sem("ht_ready"), sem("logits_done"), sem("top_ready")
        oh_turned, oht_ready = sem("oh_turned"), sem("oht_ready")
        hid_done, hid_ready, hidm_ready = sem("hid_done"), sem("hid_ready"), sem("hidm_ready")
        y_done, y_ready, y_free = sem("y_done"), sem("y_ready"), sem("y_free")

        block = ctx.enter_context(nc.Block())

        CHAIN = 38
        gu_tiles = [(n, min(4, GU - n)) for n in range(0, GU, 4)]
        gu_banks = (mm_a, mm_b, mm_c)

        @block.sync
        def _(sp):
            sp.dma_start(wq_in[:, :GU * D], w_gu.rearrange("p j d -> p (j d)")).then_inc(in_wq, 16)
            sp.dma_start(wq_in[:, GU * D:], w_down.rearrange("p j d -> p (j d)")).then_inc(in_wq, 16)
            sp.dma_start(x_s[:], x[0]).then_inc(in_x, 16)
            sp.dma_start(xt_s[:], xt[0]).then_inc(in_x, 16)
            with sp.Fori(0, CH) as c:
                sp.wait_ge(x1_ready, c + 1)
                nxt = sp.snap((c + 1) % CH)
                sp.dma_start(x_s[:], x[bass.ds(nxt, 1)].rearrange("a p d -> (a p) d")).then_inc(in_x, 16)
                sp.dma_start(xt_s[:], xt[bass.ds(nxt, 1)].rearrange("a p k t -> (a p) k t")).then_inc(in_x, 16)
                sp.wait_ge(y_ready, c + 1)
                sp.dma_start(out[bass.ds(c, 1)].rearrange("a p d -> (a p) d"), y_s[:]).then_inc(y_free, 16)
            sp.wait_ge(in_x, 32 * (CH + 1))
            sp.wait_ge(y_free, 16 * (CH + 1))

        @block.gpsimd
        def _(pool):
            pool.dma_start(cond_s[:], condt).then_inc(in_mod, 16)
            pool.dma_start(wmod[:], w_mod).then_inc(in_mod, 16)
            pool.dma_start(wr_s[:], wr).then_inc(in_rec, 16)
            pool.dma_start(wk_s[:], wk).then_inc(in_rec, 16)
            pool.dma_start(router_s[:], router).then_inc(in_moe, 16)
            pool.dma_start(rb_s[:], router_b).then_inc(in_moe, 16)
            pool.dma_start(w1_s[:], w1).then_inc(in_moe, 16)
            pool.dma_start(b1_s[:], b1).then_inc(in_moe, 16)
            pool.dma_start(w2_s[:], w2).then_inc(in_moe, 16)
            pool.dma_start(b2_s[:], b2).then_inc(in_moe, 16)
            pool.memset(ones[:], 1.0).then_inc(consts, 1)
            pool.memset(spread_a[:], 1.0).then_inc(consts, 1)
            pool.iota(iota_m[:], pattern=[[1, E]], base=-E, channel_multiplier=0,
                      allow_small_or_imprecise_dtypes=True).then_inc(consts, 1)
            pool.wait_ge(consts, 3)
            pool.affine_select(out=ident[:], in_=ones[:], pattern=[[1, P]], compare_op=ALU.is_equal,
                               fill=0.0, base=0, channel_multiplier=-1).then_inc(consts, 1)
            pool.affine_select(out=spread[:], in_=spread_a[:], pattern=[[1, HID]], compare_op=ALU.is_ge,
                               fill=0.0, base=0, channel_multiplier=-(HID // E)).then_inc(consts, 1)
            pool.wait_ge(consts, 5)
            pool.affine_select(out=spread_a[:], in_=spread[:], pattern=[[-1, HID]], compare_op=ALU.is_ge,
                               fill=0.0, base=HID // E - 1, channel_multiplier=HID // E).then_inc(consts, 1)

        @block.tensor
        def _(pe):
            pe.wait_ge(consts, 6)
            pe.wait_ge(setup_v, 1)
            for b_ in (gate_g, gate_f, gate_o):
                pe.matmul(b_[:], zeros[:, :P], zeros[:], start=True, stop=True).then_inc(setup_pe, 1)
            pe.wait_ge(setup_v, 4)
            for k in range(KD):
                mm = pe.matmul(turn_b[:, :D], ys2_b[:, k].rearrange("p b t -> p (b t)"), wmod2[:, k],
                               start=(k == 0), stop=(k == KD - 1))
            mm.then_inc(setup_pe, 1)
            pe.wait_ge(setup_v, 5)
            n = 0
            for j in range(GU):
                tb = (turn_a, mm_a)[n % 2]
                if n >= 2:
                    pe.wait_ge(wq_kept, n - 1)
                for k in range(KD):
                    mm = pe.transpose(tb[:, k * P:(k + 1) * P], wq_c[:, j * D + k * P:j * D + (k + 1) * P], ident[:])
                mm.then_inc(wq_turned, 1)
                n += 1
            for f in range(KF):
                tb = (turn_a, mm_a)[n % 2]
                rows = P if f < KF - 1 else FR
                pe.wait_ge(wq_kept, n - 1)
                for k in range(KD):
                    off = GU * D + k * FF + f * P
                    mm = pe.transpose(tb[:rows, k * P:(k + 1) * P], wq_c[:, off:off + rows], ident[:])
                mm.then_inc(wq_turned, 1)
                n += 1
            pe.wait_ge(wq_kept, n)
            pe.wait_ge(in_rec, 32)
            pe.wait_ge(in_moe, 96)

            def modulated(c):
                pe.wait_ge(xm_ready, c + 1)
                for k in range(KD):
                    mm = pe.matmul(mm_a[:, :D], xm[:, k], wmod[:, k], start=(k == 0), stop=(k == KD - 1))
                mm.then_inc(mod_done, 1)

            def gate_up(c):
                pe.wait_ge(oq_ready, c + 1)
                for k in range(KD):
                    mm = pe.transpose(turn_a[:, k * P:(k + 1) * P], oq[:, k * P:(k + 1) * P], ident[:])
                mm.then_inc(oq_turned, 1)
                pe.wait_ge(oqt_ready, c + 1)
                for (n0, w), bk in zip(gu_tiles, gu_banks):
                    for k in range(KD):
                        mm = pe.matmul(bk[:, :w * P], oq_t[:, k], wgu_t[:, k, n0 * P:(n0 + w) * P],
                                       start=(k == 0), stop=(k == KD - 1))
                    mm.then_inc(gu_done, 1)

            def down(c):
                pe.wait_ge(hq_ready, c + 1)
                for f in range(KF):
                    rows = P if f < KF - 1 else FR
                    tb = (turn_a, turn_b)[f // 4]
                    mm = pe.transpose(tb[:rows, (f % 4) * P:(f % 4 + 1) * P], hq[:, f * P:f * P + rows], ident[:])
                    if f == 3 or f == KF - 1:
                        mm.then_inc(hq_turned, 1)
                pe.wait_ge(hqt_ready, 3 * (c + 1))
                for f in range(KF):
                    rows = P if f < KF - 1 else FR
                    mm = pe.matmul(mm_a[:, :D], hq_t[:rows, f], wdown_t[:rows, f], start=(f == 0), stop=(f == KF - 1))
                mm.then_inc(down_done, 1)

            def x_product(c):
                pe.wait_ge(x1_ready, c + 1)
                for k in range(KD):
                    mm = pe.transpose(turn_a[:, k * P:(k + 1) * P], x1[:, k * P:(k + 1) * P], ident[:])
                mm.then_inc(x1_turned, 1)
                pe.wait_ge(x1t_ready, c + 1)
                for g, bk in enumerate((mm_a, mm_b, mm_c)):
                    for m in range(KD):
                        for k in range(KD):
                            mm = pe.matmul(bk[:, m * P:(m + 1) * P], wk_s[:, k, g * D + m * P:g * D + (m + 1) * P],
                                           x1_t[:, k], start=(k == 0), stop=(k == KD - 1))
                    mm.then_inc(xp_done, 1)

            def recurrent(step, s):
                col = s * KD * B
                st = step + s

                def part(bk, g, w, piece):
                    for m in range(KD):
                        for k in range(KD):
                            mm = pe.matmul(bk[:, col + m * B:col + (m + 1) * B],
                                           w[:, k, g * D + m * P:g * D + (m + 1) * P],
                                           h16[:, s % 2, piece, k], start=False, stop=True, skip_group_check=True)
                    return mm

                pe.wait_ge(hi_ready, st + 1)
                part(gate_g, 2, wr_hi, 0)
                part(gate_g, 2, wr_lo, 0)
                part(gate_f, 0, wr_hi, 0)
                part(gate_f, 0, wr_lo, 0)
                pe.wait_ge(lo_ready, st + 1)
                part(gate_g, 2, wr_hi, 1).then_inc(g_done, 1)
                part(gate_f, 0, wr_hi, 1).then_inc(f_done, 1)
                part(gate_o, 1, wr_hi, 0)
                part(gate_o, 1, wr_lo, 0)
                part(gate_o, 1, wr_hi, 1).then_inc(o_done, 1)

            def route(c):
                pe.wait_ge(ht_ready, c + 1)
                for k in range(KD):
                    pe.matmul(mm_a[:, :E], ht[:, k], router_s[:, k], start=(k == 0), stop=False)
                pe.matmul(mm_a[:, :E], ones[:1, :], rb_s[:], start=False, stop=True).then_inc(logits_done, 1)

            def experts(c):
                pe.wait_ge(top_ready, c + 1)
                pe.transpose(turn_a[:E, :P], onehot[:], ident[:]).then_inc(oh_turned, 1)
                pe.wait_ge(oht_ready, c + 1)
                pe.matmul(turn_b[:, :D], oh_t[:], b2_s[:], start=True, stop=False)

                def second(q):
                    pe.wait_ge(hidm_ready, c * (NB // GRP) + q + 1)
                    for j in range(GRP):
                        n = q * GRP + j
                        mm = pe.matmul(turn_b[:, :D], hidm[:, q % 2, j], w2_s[:, n], start=False, stop=(n == NB - 1))
                    return mm

                for q in range(NB // GRP):
                    hb, mb = (mm_b, mm_c) if q % 2 == 0 else (mm_a, turn_a)
                    if q >= 2:
                        pe.wait_ge(hidm_ready, c * (NB // GRP) + q - 1)
                    for j in range(GRP):
                        n = q * GRP + j
                        pe.matmul(mb[:, j * P:(j + 1) * P], spread_a[:, n * P:(n + 1) * P], oh_tb[:],
                                  start=True, stop=True)
                        for k in range(KD):
                            mm = pe.matmul(hb[:, j * P:(j + 1) * P], w1_s[:, k, n * P:(n + 1) * P], ht[:, k],
                                           start=(k == 0), stop=(k == KD - 1))
                    mm.then_inc(hid_done, 1)
                    if q >= 1:
                        second(q - 1)
                second(NB // GRP - 1).then_inc(y_done, 1)

            with pe.Fori(0, CH) as c:
                modulated(c)
                gate_up(c)
                down(c)
                x_product(c)
                pe.wait_ge(xp_ready, 3 * (c + 1))
                step = c * STEPS
                for s in range(STEPS):
                    recurrent(step, s)
                route(c)
                experts(c)

        @block.scalar
        def _(act):
            act.wait_ge(setup_v, 5)
            act.activation(dsq[:], dvar[:], ACT.Sqrt).then_inc(setup_act, 1)
            n = 0
            for j in range(GU):
                tb = (turn_a, mm_a)[n % 2]
                act.wait_ge(wq_turned, n + 1)
                act.activation(wgu_t[:, :, j * P:(j + 1) * P], tb[:, :D].rearrange("p (k r) -> p k r", k=KD),
                               ACT.Copy).then_inc(wq_kept, 1)
                n += 1
            for f in range(KF):
                tb = (turn_a, mm_a)[n % 2]
                rows = P if f < KF - 1 else FR
                act.wait_ge(wq_turned, n + 1)
                act.activation(wdown_t[:rows, f], tb[:rows, :D], ACT.Copy).then_inc(wq_kept, 1)
                n += 1

            def keep_oq(c):
                act.wait_ge(oq_turned, c + 1)
                act.activation(oq_t[:].rearrange("p k t -> p (k t)"), turn_a[:, :D], ACT.Copy).then_inc(oqt_ready, 1)

            def sigmoids(c):
                for i, ((n0, w), bk) in enumerate(zip(gu_tiles, gu_banks)):
                    act.wait_ge(gu_done, 3 * c + i + 1)
                    act.activation(sig[:, n0 * 64:(n0 + w) * 64].rearrange("p (j r) -> p j r", r=64),
                                   bk[:, :w * P].rearrange("p (j r) -> p j r", r=P)[:, :, :64],
                                   ACT.Sigmoid).then_inc(sig_ready, 1)

            def keep_hq(c):
                act.wait_ge(hq_turned, 2 * c + 1)
                act.activation(hq_t[:, :4].rearrange("p f t -> p (f t)"), turn_a[:], ACT.Copy).then_inc(hqt_ready, 1)
                act.wait_ge(hq_turned, 2 * c + 2)
                act.activation(hq_t[:, 4], turn_b[:, :P], ACT.Copy).then_inc(hqt_ready, 1)
                act.activation(hq_t[:FR, 5], turn_b[:FR, P:2 * P], ACT.Copy).then_inc(hqt_ready, 1)

            def keep_x1(c):
                act.wait_ge(x1_turned, c + 1)
                act.activation(x1_t[:].rearrange("p k t -> p (k t)"), turn_a[:, :D], ACT.Copy).then_inc(x1t_ready, 1)

            def gates(step, s):
                col, w = s * KD * B, KD * B
                st = step + s
                act.wait_ge(g_done, st + 1)
                act.activation(fold0[:, s % 2, 4:4 + 4 * w].rearrange("p (a b) -> p a b", b=4)[:, :, 0:2],
                               gate_g[:, col:col + w].unsqueeze(2).to_broadcast([P, w, 2]),
                               ACT.Tanh, scale=1.0 / GATE_SCALE)
                act.wait_ge(f_done, st + 1)
                act.activation(fold1[:, 4:4 + 4 * w:4], gate_f[:, col:col + w], ACT.Sigmoid,
                               scale=1.0 / GATE_SCALE).then_inc(f_ready, 1)
                act.wait_ge(o_done, st + 1)
                act.activation(so[:], gate_o[:, col:col + w], ACT.Sigmoid, scale=1.0 / GATE_SCALE)
                act.wait_ge(c_ready, st + 1)
                act.activation(tc[:], fold0[:, (s + 1) % 2, 3:3 + 4 * w:4], ACT.Tanh).then_inc(tc_ready, 1)

            def route(c):
                act.wait_ge(oh_turned, c + 1)
                act.activation(oh_tb[:], turn_a[:E, :P], ACT.Copy)
                act.activation(oh_t[:], turn_a[:E, :P], ACT.Copy).then_inc(oht_ready, 1)

            def hidden(c):
                for q in range(NB // GRP):
                    hb = mm_b if q % 2 == 0 else mm_a
                    act.wait_ge(hid_done, c * (NB // GRP) + q + 1)
                    for j in range(GRP):
                        n = q * GRP + j
                        a = act.activation(hid[:, q % 2, j], hb[:, j * P:(j + 1) * P], ACT.Relu, bias=b1_s[:, n:n + 1])
                    a.then_inc(hid_ready, 1)

            with act.Fori(0, CH) as c:
                keep_oq(c)
                sigmoids(c)
                keep_hq(c)
                keep_x1(c)
                step = c * STEPS
                for s in range(STEPS):
                    gates(step, s)
                route(c)
                hidden(c)

        @block.vector
        def _(v):
            def quantise(src, dst, c_v, c_c, c_t, nb, sm, at):
                w = nb * QB

                def blocks(t):
                    return t[:, :w].rearrange("p (n q) -> p n q", q=QB)

                def scales():
                    return q_scale[:, :nb].unsqueeze(2).to_broadcast([P, nb, QB])

                v.tensor_reduce(q_amax[:, :nb], blocks(src), AX.X, ALU.max, apply_absolute_value=True).then_inc(sm, 1)
                v.wait_ge(sm, at(1))
                v.tensor_scalar(q_scale[:, :nb], q_amax[:, :nb], 1.0 / 6.0, 1e-12, ALU.mult, ALU.max).then_inc(sm, 1)
                v.wait_ge(sm, at(2))
                v.reciprocal(q_inv[:, :nb], q_scale[:, :nb]).then_inc(sm, 1)
                v.wait_ge(sm, at(3))
                v.tensor_tensor(blocks(src), blocks(src), q_inv[:, :nb].unsqueeze(2).to_broadcast([P, nb, QB]), ALU.mult).then_inc(sm, 1)
                v.wait_ge(sm, at(4))
                v.tensor_scalar(c_v[:, :w].bitcast(I32), src[:, :w].bitcast(I32), 2 ** 31 - 1, None, ALU.bitwise_and).then_inc(sm, 1)
                v.wait_ge(sm, at(5))
                v.tensor_scalar(c_c[:, :w], c_v[:, :w], 0.25, None, ALU.is_gt).then_inc(sm, 1)
                v.tensor_scalar(c_t[:, :w], c_v[:, :w], 5.0, 2.0, ALU.is_gt, ALU.mult).then_inc(sm, 1)
                k = 7
                for i, mid in enumerate((0.75, 3.5, 1.25, 2.5, 1.75)):
                    acc = c_c if i % 2 == 0 else c_t
                    v.wait_ge(sm, at(k - 1))
                    v.scalar_tensor_tensor(acc[:, :w], c_v[:, :w], mid, acc[:, :w], ALU.is_gt, ALU.add).then_inc(sm, 1)
                    k += 1
                v.wait_ge(sm, at(12))
                v.scalar_tensor_tensor(c_v[:, :w], c_t[:, :w], 2.0, c_c[:, :w], ALU.mult, ALU.add).then_inc(sm, 1)
                v.wait_ge(sm, at(13))
                v.scalar_tensor_tensor(c_v[:, :w].bitcast(I32), src[:, :w].bitcast(I32), -2 ** 31, c_v[:, :w].bitcast(I32),
                                       ALU.bitwise_and, ALU.bitwise_or).then_inc(sm, 1)
                v.wait_ge(sm, at(14))
                return v.scalar_tensor_tensor(blocks(dst), blocks(c_v), 0.5, scales(), ALU.mult, ALU.mult)

            v.memset(zeros[:], 0.0).then_inc(setup_v, 1)
            v.memset(fold0[:], 0.0)
            v.memset(y_s[:], 0.0).then_inc(y_free, 16)
            v.memset(fold1[:], 1.0).then_inc(chain, 1)
            v.wait_ge(chain, 1)
            v.memset(fold1[:, 2::4], 0.0)
            v.wait_ge(in_mod, 32)
            v.tensor_scalar(ys[:], cond_s[:], D ** -0.5, None, ALU.mult).then_inc(setup_v, 1)
            v.wait_ge(setup_v, 2)
            v.tensor_tensor(ys2[:], ys[:], ys[:], ALU.mult).then_inc(setup_v, 1)
            v.tensor_tensor(wmod2[:], wmod[:], wmod[:], ALU.mult)
            v.wait_ge(setup_v, 3)
            v.tensor_copy(ys2_b[:], ys2[:].unsqueeze(3).to_broadcast([P, KD, B, STEPS])).then_inc(setup_v, 1)
            v.tensor_copy(fold0[:, 0, 3:3 + 4 * KD * B:4], cond_s[:].rearrange("p k b -> p (k b)"))
            v.tensor_scalar(h16[:, 0, 0], cond_s[:], H_SCALE, None, ALU.mult).then_inc(hi_ready, 1)
            v.wait_ge(hi_ready, 1)
            v.scalar_tensor_tensor(h16[:, 0, 1], cond_s[:], H_SCALE, h16[:, 0, 0], ALU.mult,
                                   ALU.subtract).then_inc(lo_ready, 1)
            v.wait_ge(in_rec, 32)
            v.tensor_scalar(wr_hi[:], wr_s[:], W_SCALE, None, ALU.mult).then_inc(chain, 1)
            v.wait_ge(chain, 2)
            v.scalar_tensor_tensor(wr_lo[:], wr_s[:], W_SCALE, wr_hi[:], ALU.mult, ALU.subtract)
            v.wait_ge(in_wq, 32)
            quantise(wq_in, wq_c, wq_v, wq_c, wq_t, WQ // QB, chain, lambda k: 2 + k).then_inc(chain, 1)
            v.wait_ge(setup_pe, 4)
            v.tensor_scalar(dvar[:], turn_b[:, :D], 1e-8, None, ALU.add).then_inc(setup_v, 1)
            v.wait_ge(setup_act, 1)
            v.reciprocal(dinv[:], dsq[:]).then_inc(chain, 1)
            v.wait_ge(chain, 18)
            v.tensor_tensor(dtmp[:], dinv[:], dinv[:], ALU.mult).then_inc(chain, 1)
            v.wait_ge(chain, 19)
            v.tensor_tensor(dtmp[:], dtmp[:], dvar[:], ALU.mult).then_inc(chain, 1)
            v.wait_ge(chain, 20)
            v.tensor_scalar(dtmp[:], dtmp[:], -0.5, 1.5, ALU.mult, ALU.add).then_inc(chain, 1)
            v.wait_ge(chain, 21)
            v.tensor_tensor(demod[:], dinv[:], dtmp[:], ALU.mult).then_inc(chain, 1)
            C0 = 22

            def modulate(c):
                v.wait_ge(in_x, 32 * (c + 1))
                v.tensor_tensor(xm[:].rearrange("p k (b t) -> p (k b) t", b=B),
                                xt_s[:].rearrange("p k (b t) -> p (k b) t", b=B),
                                ys[:].rearrange("p k b -> p (k b)").unsqueeze(2).to_broadcast([P, KD * B, STEPS]),
                                ALU.mult).then_inc(xm_ready, 1)
                v.wait_ge(mod_done, c + 1)
                v.wait_ge(chain, C0 + c * CHAIN)
                v.tensor_tensor(o_s[:], mm_a[:, :D], demod[:], ALU.mult).then_inc(chain, 1)
                v.wait_ge(chain, C0 + c * CHAIN + 1)
                quantise(o_s, oq, q_v, q_c, q_t, D // QB, chain,
                         lambda k: C0 + c * CHAIN + 1 + k).then_inc(oq_ready, 1)

            def swiglu(c):
                k0 = C0 + c * CHAIN + 15
                for i, ((n0, w), bk) in enumerate(zip(gu_tiles, gu_banks)):
                    f = slice(n0 * 64, (n0 + w) * 64)
                    both = bk[:, :w * P].rearrange("p (j r) -> p j r", r=P)
                    v.wait_ge(sig_ready, 3 * c + i + 1)
                    v.tensor_tensor(gs[:, f].rearrange("p (j r) -> p j r", r=64), both[:, :, :64],
                                    sig[:, f].rearrange("p (j r) -> p j r", r=64), ALU.mult).then_inc(chain, 1)
                    v.wait_ge(chain, k0 + 2 * i + 1)
                    v.tensor_tensor(hh[:, f].rearrange("p (j r) -> p j r", r=64), both[:, :, 64:],
                                    gs[:, f].rearrange("p (j r) -> p j r", r=64), ALU.mult).then_inc(chain, 1)
                v.wait_ge(chain, k0 + 6)
                quantise(hh, hq, q_v, q_c, q_t, FF // QB, chain, lambda k: k0 + 6 + k).then_inc(hq_ready, 1)

            def residual(c):
                v.wait_ge(down_done, c + 1)
                v.tensor_tensor(x1[:], mm_a[:, :D], x_s[:], ALU.add).then_inc(x1_ready, 1)

            def seed_gates(c):
                for i, (src, dst) in enumerate(((mm_a, gate_f), (mm_b, gate_o), (mm_c, gate_g))):
                    v.wait_ge(xp_done, 3 * c + i + 1)
                    v.tensor_scalar(dst[:, :STEPS * KD * B].rearrange("p (t m) -> p m t", t=STEPS),
                                    src[:, :KD * P].rearrange("p (m t) -> p m t", t=STEPS), GATE_SCALE, None,
                                    ALU.mult).then_inc(xp_ready, 1)

            def cell(step, s):
                w = KD * B
                st = step + s
                v.wait_ge(f_ready, st + 1)
                v.tensor_tensor_scan(fold0[:, (s + 1) % 2, 0:4 * w], fold0[:, s % 2, 2:2 + 4 * w],
                                     fold1[:, 2:2 + 4 * w], 0.0, ALU.subtract, ALU.mult).then_inc(c_ready, 1)
                v.wait_ge(tc_ready, st + 1)
                nxt = h16[:, (s + 1) % 2]
                v.scalar_tensor_tensor(nxt[:, 0].rearrange("p k b -> p (k b)"), so[:], H_SCALE, tc[:],
                                       ALU.mult, ALU.mult).then_inc(hi_ready, 1)
                v.scalar_tensor_tensor(hist[:, s].rearrange("p k b -> p (k b)"), so[:], H_SCALE, tc[:],
                                       ALU.mult, ALU.mult).then_inc(h_ready, 1)
                v.wait_ge(h_ready, st + 1)
                v.tensor_tensor(nxt[:, 1], hist[:, s], nxt[:, 0], ALU.subtract).then_inc(lo_ready, 1)

            def route(c):
                k0 = C0 + c * CHAIN + 35
                v.tensor_scalar(ht[:].rearrange("p k (b t) -> p k b t", b=B),
                                hist[:].rearrange("p t k b -> p k b t"), 1.0 / H_SCALE, None,
                                ALU.mult).then_inc(ht_ready, 1)
                v.wait_ge(logits_done, c + 1)
                v.tensor_reduce(top[:], mm_a[:, :E], AX.X, ALU.max).then_inc(chain, 1)
                v.wait_ge(chain, k0 + 1)
                v.scalar_tensor_tensor(cand[:], mm_a[:, :E], top[:, 0:1], iota_m[:], ALU.is_equal, ALU.mult).then_inc(chain, 1)
                v.wait_ge(chain, k0 + 2)
                v.tensor_reduce(first[:], cand[:], AX.X, ALU.min).then_inc(chain, 1)
                v.wait_ge(chain, k0 + 3)
                v.tensor_scalar(onehot[:], iota_m[:], first[:, 0:1], None, ALU.is_equal).then_inc(top_ready, 1)

            def mask(c):
                for q in range(NB // GRP):
                    mb = mm_c if q % 2 == 0 else turn_a
                    v.wait_ge(hid_ready, c * (NB // GRP) + q + 1)
                    v.tensor_tensor(hidm[:, q % 2].rearrange("p j t -> p (j t)"), mb[:],
                                    hid[:, q % 2].rearrange("p j t -> p (j t)"), ALU.mult).then_inc(hidm_ready, 1)

            def finish(c):
                v.wait_ge(y_done, c + 1)
                v.wait_ge(y_free, 16 * (c + 1))
                v.scalar_tensor_tensor(y_s[:], turn_b[:, :D], 0.0, x1[:], ALU.max, ALU.add).then_inc(y_ready, 1)

            with v.Fori(0, CH) as c:
                modulate(c)
                swiglu(c)
                residual(c)
                seed_gates(c)
                step = c * STEPS
                for s in range(STEPS):
                    cell(step, s)
                route(c)
                mask(c)
                finish(c)


def kernel(**inputs):
    import numpy as np
    import concourse.bacc as bacc
    from concourse.bass_utils import run_bass_kernel_spmd

    a = {k: np.ascontiguousarray(v) for k, v in inputs.items()}
    x = a["x"]
    B, S, D = x.shape
    CH, T = S * B // P, P // B
    KD = D // P
    xc = x.reshape(B, CH, T, D).transpose(1, 0, 2, 3).reshape(CH, P, D)
    FF = a["L0_ffn_w_gate"].shape[0]
    gu = np.concatenate([a["L0_ffn_w_gate"].reshape(FF // 64, 64, D), a["L0_ffn_w_up"].reshape(FF // 64, 64, D)], axis=1)
    E, _, H = a["L1_ffn_weights1"].shape

    def halves(w):
        return w.reshape(KD, P, -1).transpose(1, 0, 2)

    laid = {
        "x": xc,
        "xt": xc.transpose(0, 2, 1).reshape(CH, KD, P, P).transpose(0, 2, 1, 3),
        "condt": halves(a["cond_1024"].T),
        "w_mod": halves(a["L0_cond_weight"]),
        "w_gu": gu.transpose(1, 0, 2),
        "w_down": halves(a["L0_ffn_w_down"]),
        "wk": halves(a["L1_cond_Wk"]),
        "wr": halves(a["L1_cond_Wr"]),
        "router": halves(a["L1_ffn_router_w"].T),
        "router_b": a["L1_ffn_router_b"].reshape(1, E),
        "w1": halves(a["L1_ffn_weights1"].transpose(1, 0, 2).reshape(D, E * H)),
        "b1": a["L1_ffn_bias1"].reshape(E * H // P, P).T,
        "w2": a["L1_ffn_weights2"].reshape(E * H // P, P, D).transpose(1, 0, 2),
        "b2": a["L1_ffn_bias2"],
    }
    laid = {k: np.ascontiguousarray(v) for k, v in laid.items()}
    nc = bacc.Bacc("TRN2", target_bir_lowering=False, num_devices=1)
    args = [nc.dram_tensor(f"in_{k}", v.shape, mybir.dt.from_np(v.dtype), kind="ExternalInput").ap() for k, v in laid.items()]
    args.append(nc.dram_tensor("out", (CH, P, D), F32, kind="ExternalOutput").ap())
    build(nc, *args)
    r = run_bass_kernel_spmd(nc, [{f"in_{k}": v for k, v in laid.items()}], core_ids=[0])
    got = r.results[0]["out"]
    return got.reshape(CH, B, T, D).transpose(1, 0, 2, 3).reshape(B, S, D)
```

```python
from contextlib import ExitStack

import concourse.bass as bass
from concourse import mybir

ALU = mybir.AluOpType
ACT = mybir.ActivationFunctionType
AX = mybir.AxisListType
F32 = mybir.dt.float32
F16 = mybir.dt.float16
BF16 = mybir.dt.bfloat16
I32 = mybir.dt.int32

P = 128
QB = 16
W_SCALE = 32.0
H_SCALE = 16.0
GATE_SCALE = W_SCALE * H_SCALE


def build(nc, x, xt, condt, w_mod, w_gu, w_down, wk, wr, router, router_b, w1, b1, w2, b2, out):
    CH, _, KD, _ = xt.shape
    B = condt.shape[2]
    D = KD * P
    STEPS = P // B
    GU = w_gu.shape[1]
    FF = GU * 64
    KF = (FF + P - 1) // P
    FR = FF - (KF - 1) * P
    G3 = wk.shape[2]
    E = router.shape[2]
    HID = w1.shape[2]
    NB = HID // P
    GRP = 4
    WQ = GU * D + KD * FF

    with ExitStack() as ctx:
        def sb(name, shape, dt=F32):
            return ctx.enter_context(nc.sbuf_tensor(name, shape, dt))

        def bank(name):
            return ctx.enter_context(nc.psum_tensor(name, [P, 512], F32))

        def sem(name):
            return ctx.enter_context(nc.semaphore(name))

        gates = ctx.enter_context(nc.psum_tensor("gates", [P, 3, 512], F32))
        gate_f, gate_o, gate_g = gates[:, 0], gates[:, 1], gates[:, 2]
        turn_a, turn_b = bank("turn_a"), bank("turn_b")
        mm_a, mm_b, mm_c = bank("mm_a"), bank("mm_b"), bank("mm_c")

        wq_in = sb("wq_in", [P, WQ])
        wq_v = sb("wq_v", [P, WQ])
        wq_t = sb("wq_t", [P, WQ])
        wq_c = sb("wq_c", [P, WQ])
        wgu_t = sb("wgu_t", [P, KD, GU * P])
        wdown_t = sb("wdown_t", [P, KF, D])
        wmod = sb("wmod", [P, KD, D])
        wmod2 = sb("wmod2", [P, KD, D])
        wk_s = sb("wk_s", [P, KD, G3])
        wr_s = sb("wr_s", [P, KD, G3])
        wr_hi = sb("wr_hi", [P, KD, G3], F16)
        wr_lo = sb("wr_lo", [P, KD, G3], F16)
        router_s = sb("router_s", [P, KD, E])
        rb_s = sb("rb_s", [1, E])
        w1_s = sb("w1_s", [P, KD, HID])
        b1_s = sb("b1_s", [P, NB])
        w2_s = sb("w2_s", [P, NB, D])
        b2_s = sb("b2_s", [E, D])
        ident = sb("ident", [P, P])
        ones = sb("ones", [P, P])
        zeros = sb("zeros", [P, 512], F16)
        spread = sb("spread", [E, HID], BF16)
        spread_a = sb("spread_a", [E, HID], BF16)
        iota_m = sb("iota_m", [P, E])
        cond_s = sb("cond_s", [P, KD, B])
        ys = sb("ys", [P, KD, B])
        ys2 = sb("ys2", [P, KD, B])
        ys2_b = sb("ys2_b", [P, KD, B, STEPS])
        dvar = sb("dvar", [P, D])
        dsq = sb("dsq", [P, D])
        dinv = sb("dinv", [P, D])
        dtmp = sb("dtmp", [P, D])
        demod = sb("demod", [P, D])
        x_s = sb("x_s", [P, D])
        xt_s = sb("xt_s", [P, KD, P])
        xm = sb("xm", [P, KD, P])
        o_s = sb("o_s", [P, D])
        oq = sb("oq", [P, D])
        oq_t = sb("oq_t", [P, KD, P])
        sig = sb("sig", [P, FF])
        gs = sb("gs", [P, FF])
        hh = sb("hh", [P, FF])
        hq = sb("hq", [P, FF])
        hq_t = sb("hq_t", [P, KF, P])
        q_amax = sb("q_amax", [P, WQ // QB])
        q_inv = sb("q_inv", [P, WQ // QB])
        q_scale = sb("q_scale", [P, WQ // QB])
        q_v = sb("q_v", [P, FF])
        q_c = sb("q_c", [P, FF])
        q_t = sb("q_t", [P, FF])
        x1 = sb("x1", [P, D])
        x1_t = sb("x1_t", [P, KD, P])
        x1_prev = sb("x1_prev", [P, D])
        xp = sb("xp", [P, 3, STEPS * KD * B])
        h16 = sb("h16", [P, 2, 2, KD, B], F16)
        fold0 = sb("fold0", [P, 2, 4 * KD * B + 4])
        fold1 = sb("fold1", [P, 4 * KD * B + 4])
        so = sb("so", [P, KD * B])
        tc = sb("tc", [P, KD * B])
        hist = sb("hist", [P, STEPS, KD, B])
        ht = sb("ht", [P, KD, P])
        top = sb("top", [P, 1])
        cand = sb("cand", [P, E])
        first = sb("first", [P, 1])
        onehot = sb("onehot", [P, E])
        oh_t = sb("oh_t", [E, P])
        oh_tb = sb("oh_tb", [E, P], BF16)
        hid = sb("hid", [P, 2, GRP, P])
        hidm = sb("hidm", [P, 2, GRP, P])
        y_s = sb("y_s", [P, D])

        in_wq, in_mod, in_rec, in_moe = sem("in_wq"), sem("in_mod"), sem("in_rec"), sem("in_moe")
        in_x = sem("in_x")
        consts = sem("consts")
        setup_v = sem("setup_v")
        setup_pe = sem("setup_pe")
        setup_act = sem("setup_act")
        wq_turned, wq_kept = sem("wq_turned"), sem("wq_kept")
        chain, moe_chain = sem("chain"), sem("moe_chain")
        xm_ready, mod_done = sem("xm_ready"), sem("mod_done")
        oq_ready, oq_turned, oqt_ready = sem("oq_ready"), sem("oq_turned"), sem("oqt_ready")
        gu_done, sig_ready = sem("gu_done"), sem("sig_ready")
        hq_ready, hq_turned, hqt_ready = sem("hq_ready"), sem("hq_turned"), sem("hqt_ready")
        down_done, x1_ready, x1_turned, x1t_ready = (sem("down_done"), sem("x1_ready"),
                                                    sem("x1_turned"), sem("x1t_ready"))
        xp_done, xp_ready, seeded = sem("xp_done"), sem("xp_ready"), sem("seeded")
        g_done, f_done, o_done = sem("g_done"), sem("f_done"), sem("o_done")
        f_ready, o_ready, tc_ready = sem("f_ready"), sem("o_ready"), sem("tc_ready")
        c_ready, hi_ready, h_ready, lo_ready = sem("c_ready"), sem("hi_ready"), sem("h_ready"), sem("lo_ready")
        ht_ready, logits_done, top_ready = sem("ht_ready"), sem("logits_done"), sem("top_ready")
        oh_turned, oht_ready = sem("oh_turned"), sem("oht_ready")
        hid_done, hid_ready, hidm_ready = sem("hid_done"), sem("hid_ready"), sem("hidm_ready")
        y_done, y_ready, y_free = sem("y_done"), sem("y_ready"), sem("y_free")

        block = ctx.enter_context(nc.Block())

        CHAIN = 35
        C0 = 22
        MOE_CHAIN = 3
        SEED = 4
        NQ = NB // GRP
        gu_tiles = [(n, min(4, GU - n)) for n in range(0, GU, 4)]
        gu_banks = (mm_a, mm_b, mm_c)
        hid_banks = ((mm_b, mm_c), (mm_b, mm_c), (mm_a, turn_a), (mm_b, mm_c))

        @block.sync
        def _(sp):
            sp.dma_start(wq_in[:, :GU * D], w_gu.rearrange("p j d -> p (j d)")).then_inc(in_wq, 16)
            sp.dma_start(wq_in[:, GU * D:], w_down.rearrange("p j d -> p (j d)")).then_inc(in_wq, 16)
            sp.dma_start(x_s[:], x[0]).then_inc(in_x, 16)
            sp.dma_start(xt_s[:], xt[0]).then_inc(in_x, 16)
            sp.wait_ge(x1_ready, 1)
            sp.dma_start(x_s[:], x[1]).then_inc(in_x, 16)
            sp.dma_start(xt_s[:], xt[1]).then_inc(in_x, 16)
            with sp.Fori(0, CH) as c:
                sp.wait_ge(y_ready, c + 1)
                before = sp.snap((c + (CH - 1)) % CH)
                sp.dma_start(out[bass.ds(before, 1)].rearrange("a p d -> (a p) d"), y_s[:]).then_inc(y_free, 16)
                sp.wait_ge(x1_ready, c + 2)
                after = sp.snap((c + 2) % CH)
                sp.dma_start(x_s[:], x[bass.ds(after, 1)].rearrange("a p d -> (a p) d")).then_inc(in_x, 16)
                sp.dma_start(xt_s[:], xt[bass.ds(after, 1)].rearrange("a p k t -> (a p) k t")).then_inc(in_x, 16)
            sp.wait_ge(y_ready, CH + 1)
            sp.dma_start(out[CH - 1], y_s[:]).then_inc(y_free, 16)
            sp.wait_ge(in_x, 32 * (CH + 2))
            sp.wait_ge(y_free, 16 * (CH + 2))

        @block.gpsimd
        def _(pool):
            pool.dma_start(cond_s[:], condt).then_inc(in_mod, 16)
            pool.dma_start(wmod[:], w_mod).then_inc(in_mod, 16)
            pool.dma_start(wr_s[:], wr).then_inc(in_rec, 16)
            pool.dma_start(wk_s[:], wk).then_inc(in_rec, 16)
            pool.dma_start(router_s[:], router).then_inc(in_moe, 16)
            pool.dma_start(rb_s[:], router_b).then_inc(in_moe, 16)
            pool.dma_start(w1_s[:], w1).then_inc(in_moe, 16)
            pool.dma_start(b1_s[:], b1).then_inc(in_moe, 16)
            pool.dma_start(w2_s[:], w2).then_inc(in_moe, 16)
            pool.dma_start(b2_s[:], b2).then_inc(in_moe, 16)
            pool.memset(ones[:], 1.0).then_inc(consts, 1)
            pool.memset(spread_a[:], 1.0).then_inc(consts, 1)
            pool.iota(iota_m[:], pattern=[[1, E]], base=-E, channel_multiplier=0,
                      allow_small_or_imprecise_dtypes=True).then_inc(consts, 1)
            pool.wait_ge(consts, 3)
            pool.affine_select(out=ident[:], in_=ones[:], pattern=[[1, P]], compare_op=ALU.is_equal,
                               fill=0.0, base=0, channel_multiplier=-1).then_inc(consts, 1)
            pool.affine_select(out=spread[:], in_=spread_a[:], pattern=[[1, HID]], compare_op=ALU.is_ge,
                               fill=0.0, base=0, channel_multiplier=-(HID // E)).then_inc(consts, 1)
            pool.wait_ge(consts, 5)
            pool.affine_select(out=spread_a[:], in_=spread[:], pattern=[[-1, HID]], compare_op=ALU.is_ge,
                               fill=0.0, base=HID // E - 1, channel_multiplier=HID // E).then_inc(consts, 1)

        @block.tensor
        def _(pe):
            pe.wait_ge(consts, 6)
            pe.wait_ge(setup_v, 1)
            for b_ in (gate_g, gate_f, gate_o):
                pe.matmul(b_[:], zeros[:, :P], zeros[:], start=True, stop=True).then_inc(setup_pe, 1)
            pe.wait_ge(setup_v, 4)
            for k in range(KD):
                mm = pe.matmul(turn_b[:, :D], ys2_b[:, k].rearrange("p b t -> p (b t)"), wmod2[:, k],
                               start=(k == 0), stop=(k == KD - 1))
            mm.then_inc(setup_pe, 1)
            pe.wait_ge(setup_v, 5)
            n = 0
            for j in range(GU):
                tb = (turn_a, mm_a)[n % 2]
                if n >= 2:
                    pe.wait_ge(wq_kept, n - 1)
                for k in range(KD):
                    mm = pe.transpose(tb[:, k * P:(k + 1) * P], wq_c[:, j * D + k * P:j * D + (k + 1) * P], ident[:])
                mm.then_inc(wq_turned, 1)
                n += 1
            for f in range(KF):
                tb = (turn_a, mm_a)[n % 2]
                rows = P if f < KF - 1 else FR
                pe.wait_ge(wq_kept, n - 1)
                for k in range(KD):
                    off = GU * D + k * FF + f * P
                    mm = pe.transpose(tb[:rows, k * P:(k + 1) * P], wq_c[:, off:off + rows], ident[:])
                mm.then_inc(wq_turned, 1)
                n += 1
            pe.wait_ge(wq_kept, n)
            pe.wait_ge(in_rec, 32)
            pe.wait_ge(in_moe, 96)

            def modulated(n):
                pe.wait_ge(xm_ready, n + 1)
                for k in range(KD):
                    mm = pe.matmul(mm_a[:, :D], xm[:, k], wmod[:, k], start=(k == 0), stop=(k == KD - 1))
                mm.then_inc(mod_done, 1)

            def turn_oq(n):
                pe.wait_ge(oq_ready, n + 1)
                for k in range(KD):
                    mm = pe.transpose(turn_a[:, k * P:(k + 1) * P], oq[:, k * P:(k + 1) * P], ident[:])
                mm.then_inc(oq_turned, 1)

            def gate_up(n, i, k):
                if i == 0 and k == 0:
                    pe.wait_ge(oqt_ready, n + 1)
                (n0, w), bk = gu_tiles[i], gu_banks[i]
                mm = pe.matmul(bk[:, :w * P], oq_t[:, k], wgu_t[:, k, n0 * P:(n0 + w) * P],
                               start=(k == 0), stop=(k == KD - 1))
                if k == KD - 1:
                    mm.then_inc(gu_done, 1)

            def turn_hq(n):
                pe.wait_ge(hq_ready, n + 1)
                for f in range(KF):
                    rows = P if f < KF - 1 else FR
                    tb = (turn_a, mm_b)[f // 4]
                    mm = pe.transpose(tb[:rows, (f % 4) * P:(f % 4 + 1) * P], hq[:, f * P:f * P + rows], ident[:])
                mm.then_inc(hq_turned, 1)

            def down(n, part):
                if part == 0:
                    pe.wait_ge(hqt_ready, n + 1)
                for f in range(2 * part, 2 * part + 2):
                    rows = P if f < KF - 1 else FR
                    mm = pe.matmul(mm_a[:, :D], hq_t[:rows, f], wdown_t[:rows, f], start=(f == 0), stop=(f == KF - 1))
                if part == KF // 2 - 1:
                    mm.then_inc(down_done, 1)

            def turn_x1(n):
                pe.wait_ge(x1_ready, n + 1)
                for k in range(KD):
                    mm = pe.transpose(turn_a[:, k * P:(k + 1) * P], x1[:, k * P:(k + 1) * P], ident[:])
                mm.then_inc(x1_turned, 1)

            def x_product(n, g):
                if g == 0:
                    pe.wait_ge(x1t_ready, n + 1)
                bk = (mm_a[:, :D], mm_a[:, D:], mm_b[:, :D])[g]
                for m in range(KD):
                    for k in range(KD):
                        mm = pe.matmul(bk[:, m * P:(m + 1) * P], wk_s[:, k, g * D + m * P:g * D + (m + 1) * P],
                                       x1_t[:, k], start=(k == 0), stop=(k == KD - 1))
                if g >= 1:
                    mm.then_inc(xp_done, 1)

            def recurrent(c, s):
                col = s * KD * B
                st = c * STEPS + s

                def part(bk, g, w, piece):
                    for m in range(KD):
                        for k in range(KD):
                            mm = pe.matmul(bk[:, col + m * B:col + (m + 1) * B],
                                           w[:, k, g * D + m * P:g * D + (m + 1) * P],
                                           h16[:, s % 2, piece, k], start=False, stop=True, skip_group_check=True)
                    return mm

                if s % SEED == 0:
                    pe.wait_ge(seeded, c * (STEPS // SEED) + s // SEED + 1)
                pe.wait_ge(hi_ready, st + 1)
                part(gate_g, 2, wr_hi, 0)
                part(gate_g, 2, wr_lo, 0)
                part(gate_f, 0, wr_hi, 0)
                part(gate_f, 0, wr_lo, 0)
                pe.wait_ge(lo_ready, st + 1)
                part(gate_g, 2, wr_hi, 1).then_inc(g_done, 1)
                part(gate_f, 0, wr_hi, 1).then_inc(f_done, 1)
                part(gate_o, 1, wr_hi, 0)
                part(gate_o, 1, wr_lo, 0)
                part(gate_o, 1, wr_hi, 1).then_inc(o_done, 1)

            def route(m):
                pe.wait_ge(ht_ready, m + 1)
                for k in range(KD):
                    pe.matmul(turn_a[:, :E], ht[:, k], router_s[:, k], start=(k == 0), stop=False)
                pe.matmul(turn_a[:, :E], ones[:1, :], rb_s[:], start=False, stop=True).then_inc(logits_done, 1)

            def turn_onehot(m):
                pe.wait_ge(top_ready, m + 1)
                pe.transpose(turn_a[:E, :P], onehot[:], ident[:]).then_inc(oh_turned, 1)

            def out_bias(m):
                pe.wait_ge(oht_ready, m + 1)
                pe.matmul(turn_b[:, :D], oh_t[:], b2_s[:], start=True, stop=False, skip_group_check=True)

            def first(m, q, part):
                hb, mb = hid_banks[q]
                blocks = (range(2), range(2, 3), range(3, 4))[part]
                if part == 0:
                    for j in range(GRP):
                        b0 = (q * GRP + j) * P
                        pe.matmul(mb[:, j * P:(j + 1) * P], spread_a[:, b0:b0 + P], oh_tb[:], start=True, stop=True)
                for j in blocks:
                    b0 = (q * GRP + j) * P
                    for k in range(KD):
                        mm = pe.matmul(hb[:, j * P:(j + 1) * P], w1_s[:, k, b0:b0 + P], ht[:, k],
                                       start=(k == 0), stop=(k == KD - 1))
                if part == 2:
                    mm.then_inc(hid_done, 1)

            def second(m, q, part):
                if part == 0:
                    pe.wait_ge(hidm_ready, m * NQ + q + 1)
                for j in range(2 * part, 2 * part + 2):
                    b0 = q * GRP + j
                    mm = pe.matmul(turn_b[:, :D], hidm[:, q % 2, j], w2_s[:, b0], start=False, stop=(b0 == NB - 1),
                                   skip_group_check=True)
                if q == NQ - 1 and part == 1:
                    mm.then_inc(y_done, 1)

            def background(c, s):
                n = c + 1
                if s == 2:
                    route(c)
                elif s == 3:
                    modulated(n)
                elif s == 6:
                    turn_onehot(c)
                elif s == 8:
                    out_bias(c)
                elif s in (9, 10, 11):
                    first(c, 0, s - 9)
                elif s == 14:
                    turn_oq(n)
                elif 16 <= s < 22:
                    if s == 16:
                        pe.wait_ge(hidm_ready, c * NQ + 1)
                    gate_up(n, (s - 16) // 2, s % 2)
                elif s in (22, 23):
                    second(c, 0, s - 22)
                elif s in (25, 26, 27):
                    if s == 25:
                        pe.wait_ge(chain, C0 + n * CHAIN + 21)
                    first(c, 1, s - 25)
                elif s in (28, 29, 30):
                    first(c, 2, s - 28)
                elif s in (31, 32):
                    second(c, 1, s - 31)
                elif s in (33, 34, 35):
                    first(c, 3, s - 33)
                elif s in (36, 37):
                    second(c, 2, s - 36)
                elif s in (41, 42):
                    second(c, 3, s - 41)
                elif s == 43:
                    turn_hq(n)
                elif s in (46, 47, 48):
                    down(n, s - 46)
                elif s == 50:
                    turn_x1(n)
                elif s in (53, 54, 55):
                    x_product(n, s - 53)

            modulated(0)
            turn_oq(0)
            for i in range(len(gu_tiles)):
                for k in range(KD):
                    gate_up(0, i, k)
            turn_hq(0)
            for part in range(KF // 2):
                down(0, part)
            turn_x1(0)
            for g in range(3):
                x_product(0, g)
            with pe.Fori(0, CH) as c:
                for s in range(STEPS):
                    recurrent(c, s)
                    background(c, s)
            route(CH)
            turn_onehot(CH)
            out_bias(CH)
            for q in range(NQ):
                if q in (1, 3):
                    pe.wait_ge(hidm_ready, CH * NQ + (q + 1) // 2)
                for part in range(3):
                    first(CH, q, part)
                if q >= 1:
                    second(CH, q - 1, 0)
                    second(CH, q - 1, 1)
            second(CH, NQ - 1, 0)
            second(CH, NQ - 1, 1)

        @block.scalar
        def _(act):
            act.wait_ge(setup_v, 5)
            act.activation(dsq[:], dvar[:], ACT.Sqrt).then_inc(setup_act, 1)
            n = 0
            for j in range(GU):
                tb = (turn_a, mm_a)[n % 2]
                act.wait_ge(wq_turned, n + 1)
                act.activation(wgu_t[:, :, j * P:(j + 1) * P], tb[:, :D].rearrange("p (k r) -> p k r", k=KD),
                               ACT.Copy).then_inc(wq_kept, 1)
                n += 1
            for f in range(KF):
                tb = (turn_a, mm_a)[n % 2]
                rows = P if f < KF - 1 else FR
                act.wait_ge(wq_turned, n + 1)
                act.activation(wdown_t[:rows, f], tb[:rows, :D], ACT.Copy).then_inc(wq_kept, 1)
                n += 1

            def keep_oq(n):
                act.wait_ge(oq_turned, n + 1)
                act.activation(oq_t[:].rearrange("p k t -> p (k t)"), turn_a[:, :D], ACT.Copy).then_inc(oqt_ready, 1)

            def sigmoid(n, i):
                (n0, w), bk = gu_tiles[i], gu_banks[i]
                act.wait_ge(gu_done, 3 * n + i + 1)
                act.activation(sig[:, n0 * 64:(n0 + w) * 64].rearrange("p (j r) -> p j r", r=64),
                               bk[:, :w * P].rearrange("p (j r) -> p j r", r=P)[:, :, :64],
                               ACT.Sigmoid).then_inc(sig_ready, 1)

            def keep_hq(n, part):
                if part == 0:
                    act.wait_ge(hq_turned, n + 1)
                    act.activation(hq_t[:, :4].rearrange("p f t -> p (f t)"), turn_a[:], ACT.Copy)
                else:
                    act.activation(hq_t[:, 4], mm_b[:, :P], ACT.Copy)
                    act.activation(hq_t[:FR, 5], mm_b[:FR, P:2 * P], ACT.Copy).then_inc(hqt_ready, 1)

            def keep_x1(n):
                act.wait_ge(x1_turned, n + 1)
                act.activation(x1_t[:].rearrange("p k t -> p (k t)"), turn_a[:, :D], ACT.Copy).then_inc(x1t_ready, 1)

            def keep_xp(n, g):
                act.wait_ge(xp_done, 2 * n + max(g, 1))
                src = (mm_a[:, :D], mm_a[:, D:], mm_b[:, :D])[g]
                act.activation(xp[:, g].rearrange("p (t m b) -> p m b t", t=STEPS, m=KD),
                               src.rearrange("p (m b t) -> p m b t", m=KD, b=B), ACT.Copy,
                               scale=GATE_SCALE).then_inc(xp_ready, 1)

            def gate_functions(c, s):
                col, w = s * KD * B, KD * B
                st = c * STEPS + s
                act.wait_ge(g_done, st + 1)
                act.activation(fold0[:, s % 2, 4:4 + 4 * w].rearrange("p (a b) -> p a b", b=4)[:, :, 0:2],
                               gate_g[:, col:col + w].unsqueeze(2).to_broadcast([P, w, 2]),
                               ACT.Tanh, scale=1.0 / GATE_SCALE)
                act.wait_ge(f_done, st + 1)
                act.activation(fold1[:, 4:4 + 4 * w:4], gate_f[:, col:col + w], ACT.Sigmoid,
                               scale=1.0 / GATE_SCALE).then_inc(f_ready, 1)
                act.wait_ge(o_done, st + 1)
                act.activation(so[:], gate_o[:, col:col + w], ACT.Sigmoid, scale=1.0 / GATE_SCALE).then_inc(o_ready, 1)
                act.wait_ge(c_ready, st + 1)
                act.activation(tc[:], fold0[:, (s + 1) % 2, 3:3 + 4 * w:4], ACT.Tanh).then_inc(tc_ready, 1)

            def keep_onehot(m):
                act.wait_ge(oh_turned, m + 1)
                act.activation(oh_tb[:], turn_a[:E, :P], ACT.Copy)
                act.activation(oh_t[:], turn_a[:E, :P], ACT.Copy).then_inc(oht_ready, 1)

            def hidden(m, q, part):
                hb = hid_banks[q][0]
                if part == 0:
                    act.wait_ge(hid_done, m * NQ + q + 1)
                for j in range(2 * part, 2 * part + 2):
                    b0 = q * GRP + j
                    a = act.activation(hid[:, q % 2, j], hb[:, j * P:(j + 1) * P], ACT.Relu, bias=b1_s[:, b0:b0 + 1])
                if part == 1:
                    a.then_inc(hid_ready, 1)

            def background(c, s):
                n = c + 1
                if s == 7:
                    keep_onehot(c)
                elif s in (12, 13):
                    hidden(c, 0, s - 12)
                elif s == 15:
                    keep_oq(n)
                elif s in (18, 20, 22):
                    sigmoid(n, (s - 18) // 2)
                elif s in (28, 29):
                    hidden(c, 1, s - 28)
                elif s in (31, 32):
                    hidden(c, 2, s - 31)
                elif s in (36, 37):
                    hidden(c, 3, s - 36)
                elif s in (44, 45):
                    keep_hq(n, s - 44)
                elif s == 51:
                    keep_x1(n)
                elif s in (57, 58, 59):
                    keep_xp(n, s - 57)

            keep_oq(0)
            for i in range(len(gu_tiles)):
                sigmoid(0, i)
            keep_hq(0, 0)
            keep_hq(0, 1)
            keep_x1(0)
            for g in range(3):
                keep_xp(0, g)
            with act.Fori(0, CH) as c:
                for s in range(STEPS):
                    gate_functions(c, s)
                    background(c, s)
            keep_onehot(CH)
            for q in range(NQ):
                hidden(CH, q, 0)
                hidden(CH, q, 1)

        @block.vector
        def _(v):
            def quantise(k, src, dst, mag, half, whole, nb, base):
                w = nb * QB

                def blocks(t):
                    return t[:, :w].rearrange("p (n q) -> p n q", q=QB)

                def spread_out(t):
                    return t[:, :nb].unsqueeze(2).to_broadcast([P, nb, QB])

                v.wait_ge(chain, base + (k - 1 if 6 <= k <= 11 else k))
                if k == 0:
                    v.tensor_reduce(q_amax[:, :nb], blocks(src), AX.X, ALU.max, apply_absolute_value=True).then_inc(chain, 1)
                elif k == 1:
                    v.tensor_scalar(q_scale[:, :nb], q_amax[:, :nb], 1.0 / 6.0, 1e-12, ALU.mult, ALU.max).then_inc(chain, 1)
                elif k == 2:
                    v.reciprocal(q_inv[:, :nb], q_scale[:, :nb]).then_inc(chain, 1)
                elif k == 3:
                    v.tensor_tensor(blocks(src), blocks(src), spread_out(q_inv), ALU.mult).then_inc(chain, 1)
                elif k == 4:
                    v.tensor_scalar(mag[:, :w].bitcast(I32), src[:, :w].bitcast(I32), 2 ** 31 - 1, None,
                                    ALU.bitwise_and).then_inc(chain, 1)
                elif k == 5:
                    v.tensor_scalar(half[:, :w], mag[:, :w], 0.25, None, ALU.is_gt).then_inc(chain, 1)
                elif k == 6:
                    v.tensor_scalar(whole[:, :w], mag[:, :w], 5.0, 2.0, ALU.is_gt, ALU.mult).then_inc(chain, 1)
                elif k <= 11:
                    acc = half if k % 2 == 1 else whole
                    mid = (0.75, 3.5, 1.25, 2.5, 1.75)[k - 7]
                    v.scalar_tensor_tensor(acc[:, :w], mag[:, :w], mid, acc[:, :w], ALU.is_gt, ALU.add).then_inc(chain, 1)
                elif k == 12:
                    v.scalar_tensor_tensor(mag[:, :w], whole[:, :w], 2.0, half[:, :w], ALU.mult, ALU.add).then_inc(chain, 1)
                elif k == 13:
                    v.scalar_tensor_tensor(mag[:, :w].bitcast(I32), src[:, :w].bitcast(I32), -2 ** 31,
                                           mag[:, :w].bitcast(I32), ALU.bitwise_and, ALU.bitwise_or).then_inc(chain, 1)
                else:
                    return v.scalar_tensor_tensor(blocks(dst), blocks(mag), 0.5, spread_out(q_scale), ALU.mult, ALU.mult)

            v.memset(zeros[:], 0.0).then_inc(setup_v, 1)
            v.memset(fold0[:], 0.0)
            v.memset(y_s[:], 0.0).then_inc(y_free, 16)
            v.memset(hist[:], 0.0)
            v.memset(ht[:], 0.0)
            v.memset(x1_prev[:], 0.0)
            v.memset(fold1[:], 1.0).then_inc(chain, 1)
            v.wait_ge(chain, 1)
            v.memset(fold1[:, 2::4], 0.0)
            v.wait_ge(in_mod, 32)
            v.tensor_scalar(ys[:], cond_s[:], D ** -0.5, None, ALU.mult).then_inc(setup_v, 1)
            v.wait_ge(setup_v, 2)
            v.tensor_tensor(ys2[:], ys[:], ys[:], ALU.mult).then_inc(setup_v, 1)
            v.tensor_tensor(wmod2[:], wmod[:], wmod[:], ALU.mult)
            v.wait_ge(setup_v, 3)
            v.tensor_copy(ys2_b[:], ys2[:].unsqueeze(3).to_broadcast([P, KD, B, STEPS])).then_inc(setup_v, 1)
            v.tensor_copy(fold0[:, 0, 3:3 + 4 * KD * B:4], cond_s[:].rearrange("p k b -> p (k b)"))
            v.tensor_scalar(h16[:, 0, 0], cond_s[:], H_SCALE, None, ALU.mult).then_inc(hi_ready, 1)
            v.wait_ge(hi_ready, 1)
            v.scalar_tensor_tensor(h16[:, 0, 1], cond_s[:], H_SCALE, h16[:, 0, 0], ALU.mult,
                                   ALU.subtract).then_inc(lo_ready, 1)
            v.wait_ge(in_rec, 32)
            v.tensor_scalar(wr_hi[:], wr_s[:], W_SCALE, None, ALU.mult).then_inc(chain, 1)
            v.wait_ge(chain, 2)
            v.scalar_tensor_tensor(wr_lo[:], wr_s[:], W_SCALE, wr_hi[:], ALU.mult, ALU.subtract)
            v.wait_ge(in_wq, 32)
            for k in range(14):
                quantise(k, wq_in, wq_c, wq_v, wq_c, wq_t, WQ // QB, 2)
            quantise(14, wq_in, wq_c, wq_v, wq_c, wq_t, WQ // QB, 2).then_inc(chain, 1)
            v.wait_ge(setup_pe, 4)
            v.tensor_scalar(dvar[:], turn_b[:, :D], 1e-8, None, ALU.add).then_inc(setup_v, 1)
            v.wait_ge(setup_act, 1)
            v.reciprocal(dinv[:], dsq[:]).then_inc(chain, 1)
            v.wait_ge(chain, 18)
            v.tensor_tensor(dtmp[:], dinv[:], dinv[:], ALU.mult).then_inc(chain, 1)
            v.wait_ge(chain, 19)
            v.tensor_tensor(dtmp[:], dtmp[:], dvar[:], ALU.mult).then_inc(chain, 1)
            v.wait_ge(chain, 20)
            v.tensor_scalar(dtmp[:], dtmp[:], -0.5, 1.5, ALU.mult, ALU.add).then_inc(chain, 1)
            v.wait_ge(chain, 21)
            v.tensor_tensor(demod[:], dinv[:], dtmp[:], ALU.mult).then_inc(chain, 1)

            def modulate(n):
                v.wait_ge(in_x, 32 * (n + 1))
                v.tensor_tensor(xm[:].rearrange("p k (b t) -> p (k b) t", b=B),
                                xt_s[:].rearrange("p k (b t) -> p (k b) t", b=B),
                                ys[:].rearrange("p k b -> p (k b)").unsqueeze(2).to_broadcast([P, KD * B, STEPS]),
                                ALU.mult).then_inc(xm_ready, 1)

            def demodulate(n):
                v.wait_ge(mod_done, n + 1)
                v.tensor_tensor(o_s[:], mm_a[:, :D], demod[:], ALU.mult).then_inc(chain, 1)

            def quantise_o(n, k):
                last = quantise(k, o_s, oq, q_v, q_c, q_t, D // QB, C0 + n * CHAIN + 1)
                if k == 14:
                    last.then_inc(oq_ready, 1)

            def swiglu(n, i):
                k0 = C0 + n * CHAIN + 15
                (n0, w), bk = gu_tiles[i], gu_banks[i]
                f = slice(n0 * 64, (n0 + w) * 64)
                both = bk[:, :w * P].rearrange("p (j r) -> p j r", r=P)
                v.wait_ge(sig_ready, 3 * n + i + 1)
                v.tensor_tensor(gs[:, f].rearrange("p (j r) -> p j r", r=64), both[:, :, :64],
                                sig[:, f].rearrange("p (j r) -> p j r", r=64), ALU.mult).then_inc(chain, 1)
                v.wait_ge(chain, k0 + 2 * i + 1)
                v.tensor_tensor(hh[:, f].rearrange("p (j r) -> p j r", r=64), both[:, :, 64:],
                                gs[:, f].rearrange("p (j r) -> p j r", r=64), ALU.mult).then_inc(chain, 1)

            def quantise_h(n, k):
                last = quantise(k, hh, hq, q_v, q_c, q_t, FF // QB, C0 + n * CHAIN + 21)
                if k == 14:
                    last.then_inc(hq_ready, 1)

            def residual(n):
                v.wait_ge(down_done, n + 1)
                v.tensor_tensor(x1[:], mm_a[:, :D], x_s[:], ALU.add).then_inc(x1_ready, 1)

            def seed(s):
                w = KD * B
                v.tensor_copy(gates[:, :, s * w:(s + SEED) * w], xp[:, :, s * w:(s + SEED) * w]).then_inc(seeded, 1)

            def cell(c, s):
                w = KD * B
                st = c * STEPS + s
                v.wait_ge(f_ready, st + 1)
                v.tensor_tensor_scan(fold0[:, (s + 1) % 2, 0:4 * w], fold0[:, s % 2, 2:2 + 4 * w],
                                     fold1[:, 2:2 + 4 * w], 0.0, ALU.subtract, ALU.mult).then_inc(c_ready, 1)
                if s % SEED == 0:
                    v.wait_ge(o_ready, st + 1)
                    if s + SEED == STEPS:
                        v.wait_ge(xp_ready, 3 * (c + 2))
                    seed((s + SEED) % STEPS)
                v.wait_ge(tc_ready, st + 1)
                nxt = h16[:, (s + 1) % 2]
                v.scalar_tensor_tensor(nxt[:, 0].rearrange("p k b -> p (k b)"), so[:], H_SCALE, tc[:],
                                       ALU.mult, ALU.mult).then_inc(hi_ready, 1)
                v.scalar_tensor_tensor(hist[:, s].rearrange("p k b -> p (k b)"), so[:], H_SCALE, tc[:],
                                       ALU.mult, ALU.mult).then_inc(h_ready, 1)
                v.wait_ge(h_ready, st + 1)
                v.tensor_tensor(nxt[:, 1], hist[:, s], nxt[:, 0], ALU.subtract).then_inc(lo_ready, 1)

            def states(t0, t1):
                op = None
                for k in range(KD):
                    op = v.tensor_scalar(ht[:, k].rearrange("p (b t) -> p b t", b=B)[:, :, t0:t1],
                                         hist[:, t0:t1, k].rearrange("p t b -> p b t"), 1.0 / H_SCALE, None, ALU.mult)
                return op

            def route(m, k):
                k0 = m * MOE_CHAIN
                if k == 0:
                    v.wait_ge(logits_done, m + 1)
                    v.tensor_reduce(top[:], turn_a[:, :E], AX.X, ALU.max).then_inc(moe_chain, 1)
                    v.wait_ge(moe_chain, k0 + 1)
                    v.scalar_tensor_tensor(cand[:], turn_a[:, :E], top[:, 0:1], iota_m[:], ALU.is_equal,
                                           ALU.mult).then_inc(moe_chain, 1)
                else:
                    v.wait_ge(moe_chain, k0 + 2)
                    v.tensor_reduce(first[:], cand[:], AX.X, ALU.min).then_inc(moe_chain, 1)
                    v.wait_ge(moe_chain, k0 + 3)
                    v.tensor_scalar(onehot[:], iota_m[:], first[:, 0:1], None, ALU.is_equal).then_inc(top_ready, 1)

            def mask(m, q):
                v.wait_ge(hid_ready, m * NQ + q + 1)
                v.tensor_tensor(hidm[:, q % 2].rearrange("p j t -> p (j t)"), hid_banks[q][1][:],
                                hid[:, q % 2].rearrange("p j t -> p (j t)"), ALU.mult).then_inc(hidm_ready, 1)

            def finish(m):
                v.wait_ge(y_done, m + 1)
                v.wait_ge(y_free, 16 * (m + 1))
                v.scalar_tensor_tensor(y_s[:], turn_b[:, :D], 0.0, x1_prev[:], ALU.max, ALU.add).then_inc(y_ready, 1)

            def background(c, s):
                n = c + 1
                if s == 0:
                    states(3 * STEPS // 4, STEPS).then_inc(ht_ready, 1)
                elif s == 1:
                    modulate(n)
                elif s in (3, 4):
                    route(c, s - 3)
                elif s == 5:
                    demodulate(n)
                elif 6 <= s < 13:
                    for k in ((0, 1), (2, 3), (4, 5, 6), (7, 8), (9, 10), (11, 12), (13, 14))[s - 6]:
                        quantise_o(n, k)
                elif s == 14:
                    mask(c, 0)
                elif s in (19, 21, 23):
                    swiglu(n, (s - 19) // 2)
                elif s in (30, 33, 38):
                    mask(c, {30: 1, 33: 2, 38: 3}[s])
                elif 24 <= s < 41:
                    slots = [t for t in range(24, 41) if t not in (30, 33, 38)]
                    for k in ((0,), (1, 2), (3,), (4,), (5, 6), (7,), (8,), (9,), (10,), (11,), (12,), (13,), (14,), ())[slots.index(s)]:
                        quantise_h(n, k)
                elif s == 44:
                    finish(c)
                elif s == 46:
                    v.tensor_copy(x1_prev[:], x1[:])
                elif s == 48:
                    states(0, 3 * STEPS // 4)
                elif s == 49:
                    residual(n)

            modulate(0)
            demodulate(0)
            for k in range(15):
                quantise_o(0, k)
            for i in range(len(gu_tiles)):
                swiglu(0, i)
            for k in range(15):
                quantise_h(0, k)
            residual(0)
            v.wait_ge(xp_ready, 3)
            seed(0)
            with v.Fori(0, CH) as c:
                for s in range(STEPS):
                    cell(c, s)
                    background(c, s)
            states(3 * STEPS // 4, STEPS).then_inc(ht_ready, 1)
            route(CH, 0)
            route(CH, 1)
            for q in range(NQ):
                mask(CH, q)
            finish(CH)


def kernel(**inputs):
    import numpy as np
    import concourse.bacc as bacc
    from concourse.bass_utils import run_bass_kernel_spmd

    a = {k: np.ascontiguousarray(v) for k, v in inputs.items()}
    x = a["x"]
    B, S, D = x.shape
    CH, T = S * B // P, P // B
    KD = D // P
    xc = x.reshape(B, CH, T, D).transpose(1, 0, 2, 3).reshape(CH, P, D)
    FF = a["L0_ffn_w_gate"].shape[0]
    gu = np.concatenate([a["L0_ffn_w_gate"].reshape(FF // 64, 64, D), a["L0_ffn_w_up"].reshape(FF // 64, 64, D)], axis=1)
    E, _, H = a["L1_ffn_weights1"].shape

    def halves(w):
        return w.reshape(KD, P, -1).transpose(1, 0, 2)

    laid = {
        "x": xc,
        "xt": xc.transpose(0, 2, 1).reshape(CH, KD, P, P).transpose(0, 2, 1, 3),
        "condt": halves(a["cond_1024"].T),
        "w_mod": halves(a["L0_cond_weight"]),
        "w_gu": gu.transpose(1, 0, 2),
        "w_down": halves(a["L0_ffn_w_down"]),
        "wk": halves(a["L1_cond_Wk"]),
        "wr": halves(a["L1_cond_Wr"]),
        "router": halves(a["L1_ffn_router_w"].T),
        "router_b": a["L1_ffn_router_b"].reshape(1, E),
        "w1": halves(a["L1_ffn_weights1"].transpose(1, 0, 2).reshape(D, E * H)),
        "b1": a["L1_ffn_bias1"].reshape(E * H // P, P).T,
        "w2": a["L1_ffn_weights2"].reshape(E * H // P, P, D).transpose(1, 0, 2),
        "b2": a["L1_ffn_bias2"],
    }
    laid = {k: np.ascontiguousarray(v) for k, v in laid.items()}
    nc = bacc.Bacc("TRN2", target_bir_lowering=False, num_devices=1)
    args = [nc.dram_tensor(f"in_{k}", v.shape, mybir.dt.from_np(v.dtype), kind="ExternalInput").ap() for k, v in laid.items()]
    args.append(nc.dram_tensor("out", (CH, P, D), F32, kind="ExternalOutput").ap())
    build(nc, *args)
    r = run_bass_kernel_spmd(nc, [{f"in_{k}": v for k, v in laid.items()}], core_ids=[0])
    got = r.results[0]["out"]
    return got.reshape(CH, B, T, D).transpose(1, 0, 2, 3).reshape(B, S, D)
```

```python
from contextlib import ExitStack

import concourse.bass as bass
from concourse import mybir

ALU = mybir.AluOpType
ACT = mybir.ActivationFunctionType
AX = mybir.AxisListType
F32 = mybir.dt.float32
F16 = mybir.dt.float16
BF16 = mybir.dt.bfloat16
F32R = mybir.dt.float32r

P = 128
QB = 16
W_SCALE = 32.0
H_SCALE = 16.0
GATE_SCALE = W_SCALE * H_SCALE
HIGH, LOW = 0, 1
PARTS = ((HIGH, HIGH), (HIGH, LOW), (LOW, HIGH))


def build(nc, x, xt, condt, w_mod, w_gu, w_down, wk, wr, router, router_b, w1, b1, w2, b2, out):
    CH, _, KD, _ = xt.shape
    B = condt.shape[2]
    D = KD * P
    STEPS = P // B
    GU = w_gu.shape[1]
    FF = GU * 64
    KF = (FF + P - 1) // P
    FR = FF - (KF - 1) * P
    G3 = wk.shape[2]
    E = router.shape[2]
    HID = w1.shape[2]
    NB = HID // P
    GRP = 4
    PIECE = 3 * D
    STAGE = 4 * D

    with ExitStack() as ctx:
        def sb(name, shape, dt=F32):
            return ctx.enter_context(nc.sbuf_tensor(name, shape, dt))

        def bank(name):
            return ctx.enter_context(nc.psum_tensor(name, [P, 512], F32))

        def sem(name):
            return ctx.enter_context(nc.semaphore(name))

        gates = ctx.enter_context(nc.psum_tensor("gates", [P, 3, 512], F32))
        gate_f, gate_o, gate_g = gates[:, 0], gates[:, 1], gates[:, 2]
        turn_a, turn_b = bank("turn_a"), bank("turn_b")
        mm_a, mm_b, mm_c = bank("mm_a"), bank("mm_b"), bank("mm_c")

        wgu_t = sb("wgu_t", [P, 2, KD, GU * P], F32R)
        wdown_t = sb("wdown_t", [P, 2, KF, D], F32R)
        wmod_r = sb("wmod_r", [P, 2, KD, D], F32R)
        wmod2 = sb("wmod2", [P, KD, D])
        wk_r = sb("wk_r", [P, 2, KD, G3], F32R)
        wr_h = sb("wr_h", [P, 2, KD, G3], F16)
        w1_h = sb("w1_h", [P, 2, KD, HID], F16)
        w2_r = sb("w2_r", [P, 2, NB, D], F32R)
        router_s = sb("router_s", [P, KD, E])
        rb_s = sb("rb_s", [P, E])
        router_h = sb("router_h", [P, 2, KD, E], F16)
        b1_s = sb("b1_s", [P, NB])
        b2_s = sb("b2_s", [E, D])
        b2_r = sb("b2_r", [E, 2, D], F32R)
        stage = sb("stage", [P, 2, STAGE])
        ident = sb("ident", [P, P])
        ones = sb("ones", [P, P])
        zeros = sb("zeros", [P, 512], F16)
        spread = sb("spread", [E, HID], BF16)
        iota_m = sb("iota_m", [P, E])
        cond_s = sb("cond_s", [P, KD, B])
        ys = sb("ys", [P, KD, B])
        ys2 = sb("ys2", [P, KD, B])
        demod = sb("demod", [P, D])
        x_s = sb("x_s", [P, D])
        xt_s = sb("xt_s", [P, KD, P])
        xm = sb("xm", [P, KD, P])
        xm_r = sb("xm_r", [P, 2, KD, P], F32R)
        o_s = sb("o_s", [P, D])
        oq = sb("oq", [P, D])
        turned = sb("turned", [P, KF * P])
        oq_t = sb("oq_t", [P, 2, KD, P], F32R)
        sig = sb("sig", [P, PIECE])
        gs = sb("gs", [P, PIECE])
        hh = sb("hh", [P, PIECE])
        hq = sb("hq", [P, PIECE])
        hq_odd = sb("hq_odd", [P, PIECE])
        hq_t = sb("hq_t", [P, 2, KF, P], F32R)
        q_amax = sb("q_amax", [P, PIECE // QB])
        q_inv = sb("q_inv", [P, PIECE // QB])
        q_scale = sb("q_scale", [P, PIECE // QB])
        q_mag = sb("q_mag", [P, PIECE])
        q_half = sb("q_half", [P, PIECE])
        q_whole = sb("q_whole", [P, PIECE])
        q_signed = sb("q_signed", [P, PIECE])
        x1 = sb("x1", [P, D])
        x1_prev = sb("x1_prev", [P, D])
        x1_old = sb("x1_old", [P, D])
        x1_t = sb("x1_t", [P, KD, 2, P], F32R)
        xp = sb("xp", [P, 3, STEPS * KD * B])
        h16 = sb("h16", [P, 2, 2, KD, B], F16)
        fold0 = sb("fold0", [P, 2, 4 * KD * B + 4])
        fold1 = sb("fold1", [P, 4 * KD * B + 4])
        so = sb("so", [P, KD * B])
        tc = sb("tc", [P, KD * B])
        hist = sb("hist", [P, STEPS, KD, B])
        ht_h = sb("ht_h", [P, 2, KD, P], F16)
        logits = sb("logits", [P, E])
        top = sb("top", [P, 1])
        cand = sb("cand", [P, E])
        first = sb("first", [P, 1])
        onehot = sb("onehot", [P, E])
        oh_t = sb("oh_t", [E, P], F32R)
        oh_tb = sb("oh_tb", [E, P], BF16)
        hid = sb("hid", [P, 2, GRP, P])
        hid_r = sb("hid_r", [P, 2, 2, GRP, P], F32R)
        y_s = sb("y_s", [P, D])
        ys2_b = hid[:, 0]
        dvar, dsq, dinv = gs[:, :D], gs[:, D:2 * D], gs[:, 2 * D:3 * D]
        dtmp = o_s[:]

        in_wq = (sem("in_wq_even"), sem("in_wq_odd"))
        in_stage = (sem("in_stage_even"), sem("in_stage_odd"))
        in_cond, in_small, in_x, in_xt = sem("in_cond"), sem("in_small"), sem("in_x"), sem("in_xt")
        consts = sem("consts")
        setup_v = sem("setup_v")
        setup_pe = sem("setup_pe")
        setup_act = sem("setup_act")
        stage_high, stage_split, small_high, small_split = (sem("stage_high"), sem("stage_split"),
                                                            sem("small_high"), sem("small_split"))
        wq_ready, wq_turned, wq_high, wq_split = sem("wq_ready"), sem("wq_turned"), sem("wq_high"), sem("wq_split")
        chain, moe_chain = sem("chain"), sem("moe_chain")
        xm_ready, xm_high, xm_split, mod_done = sem("xm_ready"), sem("xm_high"), sem("xm_split"), sem("mod_done")
        abs_ready, sign_ready, signed_ready = sem("abs_ready"), sem("sign_ready"), sem("signed_ready")
        oq_ready, oq_turned, oq_high, oq_split = sem("oq_ready"), sem("oq_turned"), sem("oq_high"), sem("oq_split")
        gu_done, sig_ready = sem("gu_done"), sem("sig_ready")
        hq_ready, hq_turned, hq_high, hq_split = sem("hq_ready"), sem("hq_turned"), sem("hq_high"), sem("hq_split")
        down_done, x1_ready, x1_turned = sem("down_done"), sem("x1_ready"), sem("x1_turned")
        x1_high, x1_split = sem("x1_high"), sem("x1_split")
        xp_done, xp_half, xp_ready, seeded = sem("xp_done"), sem("xp_half"), sem("xp_ready"), sem("seeded")
        g_done, f_done, o_done = sem("g_done"), sem("f_done"), sem("o_done")
        f_ready, o_ready, tc_ready = sem("f_ready"), sem("o_ready"), sem("tc_ready")
        c_ready, hi_ready, h_ready, lo_ready = sem("c_ready"), sem("hi_ready"), sem("h_ready"), sem("lo_ready")
        ht_high, ht_split = sem("ht_high"), sem("ht_split")
        logits_done, top_ready = sem("logits_done"), sem("top_ready")
        oh_turned, oht_ready = sem("oh_turned"), sem("oht_ready")
        hid_done, hid_ready, hid_masked = sem("hid_done"), sem("hid_ready"), sem("hid_masked")
        hid_high, hid_split = sem("hid_high"), sem("hid_split")
        y_done, y_ready, y_free = sem("y_done"), sem("y_ready"), sem("y_free")

        block = ctx.enter_context(nc.Block())

        pieces = []
        for j in range(0, GU, 3):
            tiles = min(3, GU - j)
            pieces.append((w_gu[:, j:j + tiles].rearrange("p j d -> p (j d)"), tiles * D, (j, tiles), None))
        for k in range(KD):
            pieces.append((w_down[:, k], FF, None, k))
        NW = len(pieces)
        stages = []
        for raw, parts in ((w_mod, wmod_r), (wr, wr_h), (wk, wk_r), (w1, w1_h), (w2, w2_r)):
            flat = raw.rearrange("p k n -> p (k n)")
            high = parts[:, HIGH].rearrange("p k n -> p (k n)")
            low = parts[:, LOW].rearrange("p k n -> p (k n)")
            for a in range(0, flat.shape[1], STAGE):
                b_ = min(a + STAGE, flat.shape[1])
                stages.append((flat[:, a:b_], b_ - a, high[:, a:b_], low[:, a:b_], parts.dtype == F16))
        NS = len(stages)

        STEPS_Q = 12
        CHAIN = 1 + STEPS_Q + 6 + STEPS_Q
        GATED = 1 + STEPS_Q + 6
        GUW = NW - KD
        O0 = 1 + GUW * STEPS_Q + 5 + 1
        C0 = 1 + NW * STEPS_Q + 5
        MOE_CHAIN = 4
        SEED = 4
        NQ = NB // GRP
        gu_tiles = [(n, min(4, GU - n)) for n in range(0, GU, 4)]
        gu_banks = (mm_a, mm_b, mm_c)
        hid_banks = ((mm_b, mm_c), (mm_a, mm_c), (turn_a, mm_c), (mm_a, mm_b))

        def turn_banks(i):
            return (turn_a, turn_b) if i >= GUW else ((turn_a, mm_a), (mm_b, mm_c))[i % 2]

        def place(i):
            return (i, 1 + i * STEPS_Q) if i < GUW else (i + 1, O0 + (i - GUW + 1) * STEPS_Q)


        @block.sync
        def _(sp):
            def load_stage(i):
                raw, w, *_ = stages[i]
                if i >= 2:
                    sp.wait_ge(stage_split, i - 1)
                sp.dma_start(stage[:, i % 2, :w], raw).then_inc(in_stage[i % 2], 16)

            def load_wq(i):
                raw, w, _, _ = pieces[i]
                if i >= 2:
                    sp.wait_ge(wq_ready, i - 1)
                sp.dma_start((sig, hh)[i % 2][:, :w], raw).then_inc(in_wq[i % 2], 16)

            sp.dma_start(cond_s[:], condt).then_inc(in_cond, 16)
            load_wq(0)
            load_stage(0)
            load_wq(1)
            load_stage(1)
            sp.dma_start(xt_s[:], xt[0]).then_inc(in_xt, 16)
            sp.dma_start(x_s[:], x[0]).then_inc(in_x, 16)
            sp.dma_start(router_s[:], router).then_inc(in_small, 16)
            sp.dma_start(rb_s[:], router_b).then_inc(in_small, 16)
            sp.dma_start(b1_s[:], b1).then_inc(in_small, 16)
            sp.dma_start(b2_s[:], b2).then_inc(in_small, 16)
            load_stage(2)
            load_stage(3)
            load_wq(2)
            for i in range(4, NS):
                load_stage(i)
                if i % 2 == 0 and 3 + (i - 6) // 2 < NW and i >= 6:
                    load_wq(3 + (i - 6) // 2)
            sp.wait_ge(xm_ready, 1)
            sp.dma_start(xt_s[:], xt[1]).then_inc(in_xt, 16)
            sp.wait_ge(x1_ready, 1)
            sp.dma_start(x_s[:], x[1]).then_inc(in_x, 16)
            sp.wait_ge(xm_ready, 2)
            sp.dma_start(xt_s[:], xt[2]).then_inc(in_xt, 16)
            with sp.Fori(0, CH) as c:
                sp.wait_ge(x1_ready, c + 2)
                after = sp.snap((c + 2) % CH)
                sp.dma_start(x_s[:], x[bass.ds(after, 1)].rearrange("a p d -> (a p) d")).then_inc(in_x, 16)
                sp.wait_ge(xm_ready, c + 3)
                later = sp.snap((c + 3) % CH)
                sp.dma_start(xt_s[:], xt[bass.ds(later, 1)].rearrange("a p k t -> (a p) k t")).then_inc(in_xt, 16)
                sp.wait_ge(y_ready, c + 1)
                before = sp.snap((c + (CH - 1)) % CH)
                sp.dma_start(out[bass.ds(before, 1)].rearrange("a p d -> (a p) d"), y_s[:]).then_inc(y_free, 16)
            sp.wait_ge(y_ready, CH + 1)
            sp.dma_start(out[CH - 1], y_s[:]).then_inc(y_free, 16)
            sp.wait_ge(in_x, 16 * (CH + 2))
            sp.wait_ge(in_xt, 16 * (CH + 3))
            sp.wait_ge(y_free, 16 * (CH + 2))

        @block.gpsimd
        def _(pool):
            pool.memset(ones[:], 1.0).then_inc(consts, 1)
            pool.memset(spread[:], 1.0).then_inc(consts, 1)
            pool.iota(iota_m[:], pattern=[[1, E]], base=-E, channel_multiplier=0,
                      allow_small_or_imprecise_dtypes=True).then_inc(consts, 1)
            pool.wait_ge(consts, 3)
            pool.affine_select(out=ident[:], in_=ones[:], pattern=[[1, P]], compare_op=ALU.is_equal,
                               fill=0.0, base=0, channel_multiplier=-1).then_inc(consts, 1)
            pool.affine_select(out=spread[:], in_=spread[:], pattern=[[1, HID]], compare_op=ALU.is_ge,
                               fill=0.0, base=0, channel_multiplier=-(HID // E)).then_inc(consts, 1)
            pool.wait_ge(consts, 5)
            pool.affine_select(out=spread[:], in_=spread[:], pattern=[[-1, HID]], compare_op=ALU.is_ge,
                               fill=0.0, base=HID // E - 1, channel_multiplier=HID // E).then_inc(consts, 1)

            def low(dst, whole, high):
                return pool.tensor_tensor(dst, whole, high, ALU.subtract)

            def signed(base, i, w):
                pool.wait_ge(sign_ready, i + 1)
                pool.wait_ge(chain, base + 2)
                nb = w // QB
                both = q_signed[:, :w].rearrange("p (n q) -> p n q", q=QB)
                pool.tensor_tensor(both, both, q_scale[:, :nb].unsqueeze(2).to_broadcast([P, nb, QB]),
                                   ALU.mult).then_inc(signed_ready, 1)

            def split_stage(i):
                raw, w, hi, lo, scaled = stages[i]
                if i == 0:
                    pool.wait_ge(in_stage[0], 16)
                    pool.tensor_tensor(wmod2[:].rearrange("p k n -> p (k n)"), stage[:, 0, :w], stage[:, 0, :w],
                                       ALU.mult).then_inc(consts, 1)
                pool.wait_ge(stage_high, i + 1)
                low(lo, stage[:, i % 2, :w], hi if scaled else hi.bitcast(F32)).then_inc(stage_split, 1)

            def xm_low(n):
                pool.wait_ge(xm_high, n + 1)
                low(xm_r[:, LOW], xm[:], xm_r[:, HIGH].bitcast(F32)).then_inc(xm_split, 1)

            def signed_o(n):
                if n is None:
                    signed(O0, GUW, D)
                else:
                    signed(C0 + n * CHAIN + 1, NW + 2 * n, D)

            def oq_low(n):
                pool.wait_ge(oq_high, n + 1)
                low(oq_t[:, LOW].rearrange("p k t -> p (k t)"), turned[:, :D],
                    oq_t[:, HIGH].rearrange("p k t -> p (k t)").bitcast(F32)).then_inc(oq_split, 1)

            def signed_h(n):
                signed(C0 + n * CHAIN + GATED, NW + 2 * n + 1, FF)

            def hq_low(n):
                pool.wait_ge(hq_high, n + 1)
                w = (KF - 1) * P
                low(hq_t[:, LOW, :KF - 1].rearrange("p f t -> p (f t)"), turned[:, :w],
                    hq_t[:, HIGH, :KF - 1].rearrange("p f t -> p (f t)").bitcast(F32))
                low(hq_t[:FR, LOW, KF - 1], turned[:FR, w:], hq_t[:FR, HIGH, KF - 1].bitcast(F32)).then_inc(hq_split, 1)

            def x1_low(n):
                pool.wait_ge(x1_high, n + 1)
                low(x1_t[:, :, LOW], turned[:, :D].rearrange("p (k t) -> p k t", k=KD),
                    x1_t[:, :, HIGH].bitcast(F32)).then_inc(x1_split, 1)

            def hid_low(m, q):
                pool.wait_ge(hid_high, m * NQ + q + 1)
                low(hid_r[:, q % 2, LOW], hid[:, q % 2], hid_r[:, q % 2, HIGH].bitcast(F32)).then_inc(hid_split, 1)

            split_stage(0)
            for i in range(NW):
                if i == GUW:
                    signed_o(None)
                    oq_low(0)
                at, base = place(i)
                signed(base, at, pieces[i][1])
                if i == 2:
                    xm_low(0)
                for j in range(2 * i + 1, min(2 * i + 3, NS)):
                    split_stage(j)
            pool.wait_ge(small_high, 2)
            low(router_h[:, LOW], router_s[:], router_h[:, HIGH])
            low(b2_r[:, LOW], b2_s[:], b2_r[:, HIGH].bitcast(F32)).then_inc(small_split, 1)
            signed_h(0)
            hq_low(0)
            x1_low(0)
            xm_low(1)
            with pool.Fori(0, CH) as c:
                signed_o(c + 1)
                hid_low(c, 0)
                oq_low(c + 1)
                hid_low(c, 1)
                signed_h(c + 1)
                hid_low(c, 2)
                hq_low(c + 1)
                hid_low(c, 3)
                x1_low(c + 1)
                xm_low(c + 2)
            for q in range(NQ):
                hid_low(CH, q)

        @block.tensor
        def _(pe):
            pe.wait_ge(consts, 6)
            pe.wait_ge(setup_v, 1)
            for b_ in (gate_g, gate_f, gate_o):
                pe.matmul(b_[:], zeros[:, :P], zeros[:], start=True, stop=True).then_inc(setup_pe, 1)
            pe.wait_ge(setup_v, 5)
            pe.wait_ge(consts, 7)
            for k in range(KD):
                mm = pe.matmul(turn_b[:, :D], ys2_b[:, k], wmod2[:, k], start=(k == 0), stop=(k == KD - 1))
            mm.then_inc(setup_pe, 1)
            def turn_weights(i):
                _, w, _, _ = pieces[i]
                src = (hq, hq_odd)[i % 2]
                pe.wait_ge(wq_ready, i + 1)
                if i >= 2:
                    pe.wait_ge(wq_split, i if i > GUW else i - 1)
                for j in range((w + P - 1) // P):
                    rows = min(P, w - j * P)
                    tb = turn_banks(i)[j // 4]
                    mm = pe.transpose(tb[:rows, (j % 4) * P:(j % 4 + 1) * P], src[:, j * P:j * P + rows], ident[:])
                mm.then_inc(wq_turned, 1)
            def modulated(n, k):
                if k == 0:
                    pe.wait_ge(xm_split, n + 1)
                for i, (a, w) in enumerate(PARTS):
                    mm = pe.matmul(mm_a[:, :D], xm_r[:, a, k], wmod_r[:, w, k], start=(k == 0 and i == 0),
                                   stop=(k == KD - 1 and i == 2))
                if k == KD - 1:
                    mm.then_inc(mod_done, 1)

            def turn_oq(n):
                pe.wait_ge(oq_ready, n + 1)
                for k in range(KD):
                    mm = pe.transpose(turn_a[:, k * P:(k + 1) * P], oq[:, k * P:(k + 1) * P], ident[:])
                mm.then_inc(oq_turned, 1)

            def gate_up(n, i, part):
                (n0, w), bk = gu_tiles[i], gu_banks[i]
                steps = [(k, a, b_) for k in range(KD) for a, b_ in PARTS]
                if i == 0 and part == 0:
                    pe.wait_ge(oq_split, n + 1)
                if w == 4:
                    a0, a1, at, parts = part // 2 * D, part // 2 * D + D, part % 2 * 3, 4
                    todo = steps[at:at + 3]
                else:
                    a0, a1, at, parts = 0, w * P, 2 * part, 3
                    todo = steps[at:at + 2]
                for j, (k, a, b_) in enumerate(todo, at):
                    mm = pe.matmul(bk[:, a0:a1], oq_t[:, a, k], wgu_t[:, b_, k, n0 * P + a0:n0 * P + a1],
                                   start=(j == 0), stop=(j == len(steps) - 1))
                if part == parts - 1:
                    mm.then_inc(gu_done, 1)

            def turn_hq(n, part):
                if part == 0:
                    pe.wait_ge(hq_ready, n + 1)
                for f in range(3 * part, 3 * part + 3):
                    rows = P if f < KF - 1 else FR
                    tb = (turn_a, mm_c)[part]
                    mm = pe.transpose(tb[:rows, (f % 3) * P:(f % 3 + 1) * P], hq[:, f * P:f * P + rows], ident[:])
                mm.then_inc(hq_turned, 1)

            down_steps = [(a, b_, f) for f in range(KF) for a, b_ in PARTS[:2]] + [(LOW, HIGH, f) for f in range(KF)]

            def down(n, part):
                if part == 0:
                    pe.wait_ge(hq_high, n + 1)
                if part == 4:
                    pe.wait_ge(hq_split, n + 1)
                for i in range(3 * part, 3 * part + 3):
                    a, b_, f = down_steps[i]
                    rows = P if f < KF - 1 else FR
                    mm = pe.matmul(mm_a[:, :D], hq_t[:rows, a, f], wdown_t[:rows, b_, f], start=(i == 0),
                                   stop=(i == 3 * KF - 1))
                if part == KF - 1:
                    mm.then_inc(down_done, 1)

            def turn_x1(n):
                pe.wait_ge(x1_ready, n + 1)
                for k in range(KD):
                    mm = pe.transpose(turn_a[:, k * P:(k + 1) * P], x1[:, k * P:(k + 1) * P], ident[:])
                mm.then_inc(x1_turned, 1)

            def x_product(n, g, m):
                if g == 0 and m == 0:
                    pe.wait_ge(x1_split, n + 1)
                bk = (mm_a, mm_b, mm_c)[g][:, m * 2 * P:(m + 1) * 2 * P]
                cols = slice(g * D + m * P, g * D + (m + 1) * P)
                for k in range(KD):
                    pe.matmul(bk, wk_r[:, HIGH, k, cols], x1_t[:, k].rearrange("p a t -> p (a t)"),
                              start=(k == 0), stop=False, skip_group_check=True)
                    mm = pe.matmul(bk[:, :P], wk_r[:, LOW, k, cols], x1_t[:, k, HIGH],
                                   start=False, stop=(k == KD - 1), skip_group_check=True)
                if m == KD - 1:
                    mm.then_inc(xp_done, 1)

            def recurrent(c, s):
                col = s * KD * B
                st = c * STEPS + s

                def part(bk, g, w, piece):
                    for m in range(KD):
                        for k in range(KD):
                            mm = pe.matmul(bk[:, col + m * B:col + (m + 1) * B],
                                           wr_h[:, w, k, g * D + m * P:g * D + (m + 1) * P],
                                           h16[:, s % 2, piece, k], start=False, stop=True, skip_group_check=True)
                    return mm

                if s % SEED == 0:
                    pe.wait_ge(seeded, c * (STEPS // SEED) + s // SEED + 1)
                pe.wait_ge(hi_ready, st + 1)
                part(gate_g, 2, HIGH, HIGH)
                part(gate_g, 2, LOW, HIGH)
                part(gate_f, 0, HIGH, HIGH)
                part(gate_f, 0, LOW, HIGH)
                pe.wait_ge(lo_ready, st + 1)
                part(gate_g, 2, HIGH, LOW).then_inc(g_done, 1)
                part(gate_f, 0, HIGH, LOW).then_inc(f_done, 1)
                part(gate_o, 1, HIGH, HIGH)
                part(gate_o, 1, LOW, HIGH)
                part(gate_o, 1, HIGH, LOW).then_inc(o_done, 1)

            def route(m):
                pe.wait_ge(ht_split, 2 * m + 1)
                for k in range(KD):
                    for i, (a, w) in enumerate(PARTS):
                        mm = pe.matmul(turn_a[:, :E], ht_h[:, a, k], router_h[:, w, k], start=(k == 0 and i == 0),
                                       stop=(k == KD - 1 and i == 2))
                mm.then_inc(logits_done, 1)

            def turn_onehot(m):
                pe.wait_ge(top_ready, m + 1)
                pe.transpose(turn_a[:E, :P], onehot[:], ident[:]).then_inc(oh_turned, 1)

            def out_bias(m):
                pe.wait_ge(oht_ready, m + 1)
                for w in (HIGH, LOW):
                    pe.matmul(turn_b[:, :D], oh_t[:], b2_r[:, w], start=(w == HIGH), stop=False, skip_group_check=True)

            def masks(q, blocks):
                for j in blocks:
                    b0 = (q * GRP + j) * P
                    mm = pe.matmul(hid_banks[q][1][:, j * P:(j + 1) * P], spread[:, b0:b0 + P], oh_tb[:],
                                   start=True, stop=True)
                if blocks[-1] == GRP - 1:
                    mm.then_inc(hid_done, 1)

            def first(q, j, halves=range(KD)):
                b0 = (q * GRP + j) * P
                for k in halves:
                    for i, (a, w) in enumerate(PARTS):
                        pe.matmul(hid_banks[q][0][:, j * P:(j + 1) * P], w1_h[:, w, k, b0:b0 + P], ht_h[:, a, k],
                                  start=(k == 0 and i == 0), stop=(k == KD - 1 and i == 2))

            def second(m, q, j):
                if j == 0:
                    pe.wait_ge(hid_split, m * NQ + q + 1)
                b0 = q * GRP + j
                for i, (a, w) in enumerate(PARTS):
                    mm = pe.matmul(turn_b[:, :D], hid_r[:, q % 2, a, j], w2_r[:, w, b0], start=False,
                                   stop=(b0 == NB - 1 and i == 2), skip_group_check=True)
                if b0 == NB - 1:
                    mm.then_inc(y_done, 1)

            def background(c, s):
                n = c + 1
                if s in (0, 2):
                    modulated(n, s // 2)
                elif s == 1:
                    route(c)
                    first(0, 0, (0,))
                elif s == 3:
                    first(0, 0, (1,))
                    first(0, 1, (0,))
                elif s == 4:
                    first(0, 1, (1,))
                    turn_onehot(c)
                elif s in (5, 6):
                    first(0, s - 3)
                elif s == 7:
                    pe.wait_ge(chain, C0 + n * CHAIN + 1)
                    first(1, 0, (0,))
                    pe.wait_ge(oht_ready, c + 1)
                    masks(0, range(GRP))
                elif s == 8:
                    out_bias(c)
                elif s in (9, 10, 11):
                    first(1, s - 9, (1,))
                    first(1, s - 8, (0,))
                elif s == 12:
                    first(1, 3, (1,))
                    pe.wait_ge(hid_masked, c * NQ + 1)
                    masks(1, range(GRP))
                elif s == 13:
                    turn_oq(n)
                elif s in (14, 15):
                    second(c, 0, s - 14)
                elif 16 <= s < 27:
                    if s == 16:
                        pe.wait_ge(hid_masked, c * NQ + 2)
                    gate_up(n, (s - 16) // 4, s % 4)
                elif s in (27, 28):
                    second(c, 0, s - 25)
                elif 29 <= s < 33:
                    if s == 29:
                        pe.wait_ge(chain, C0 + n * CHAIN + GATED)
                    first(2, s - 29)
                    masks(2, (s - 29,))
                elif 33 <= s < 37:
                    second(c, 1, s - 33)
                elif 37 <= s < 41:
                    first(3, s - 37)
                    masks(3, (s - 37,))
                elif s in (41, 42):
                    if s == 41:
                        pe.wait_ge(hid_masked, c * NQ + 3)
                    turn_hq(n, s - 41)
                elif s == 43:
                    second(c, 2, 0)
                elif 44 <= s < 50:
                    if s == 44:
                        pe.wait_ge(hid_masked, c * NQ + 4)
                    down(n, s - 44)
                elif s == 50:
                    second(c, 2, 1)
                elif s == 51:
                    turn_x1(n)
                elif s in (52, 53):
                    second(c, 2, s - 50)
                elif 54 <= s < 60:
                    x_product(n, (s - 54) // 2, s % 2)
                else:
                    second(c, 3, s - 60)

            for i in range(GUW):
                turn_weights(i)
            pe.wait_ge(stage_split, 1)
            pe.wait_ge(wq_split, GUW - 1)
            for k in range(KD):
                modulated(0, k)
            turn_oq(0)
            pe.wait_ge(wq_split, GUW)
            for i in range(len(gu_tiles)):
                for part in range(min(4, gu_tiles[i][1])):
                    gate_up(0, i, part)
            for i in range(GUW, NW):
                turn_weights(i)
            pe.wait_ge(wq_split, NW)
            for part in range(2):
                turn_hq(0, part)
            for part in range(KF):
                down(0, part)
            turn_x1(0)
            pe.wait_ge(stage_split, NS)
            for g in range(3):
                for m in range(KD):
                    x_product(0, g, m)
            pe.wait_ge(small_split, 1)
            pe.wait_ge(in_small, 64)
            with pe.Fori(0, CH) as c:
                for s in range(STEPS):
                    recurrent(c, s)
                    background(c, s)
            route(CH)
            for j in range(GRP):
                first(0, j)
            turn_onehot(CH)
            out_bias(CH)
            masks(0, range(GRP))
            for j in range(GRP):
                first(1, j)
            for q in range(1, NQ):
                pe.wait_ge(hid_masked, CH * NQ + q)
                masks(q, range(GRP))
                if q + 1 < NQ:
                    for j in range(GRP):
                        first(q + 1, j)
                for j in range(GRP):
                    second(CH, q - 1, j)
            for j in range(GRP):
                second(CH, NQ - 1, j)

        @block.scalar
        def _(act):
            def high_stage(i):
                raw, w, hi, lo, scaled = stages[i]
                act.wait_ge(in_stage[i % 2], 16 * (i // 2 + 1))
                if scaled:
                    act.activation(hi, stage[:, i % 2, :w], ACT.Copy, scale=W_SCALE)
                    act.activation(stage[:, i % 2, :w], stage[:, i % 2, :w], ACT.Copy,
                                   scale=W_SCALE).then_inc(stage_high, 1)
                else:
                    act.activation(hi, stage[:, i % 2, :w], ACT.Copy).then_inc(stage_high, 1)

            def absolute(src, w):
                act.activation(q_mag[:, :w], src[:, :w], ACT.Abs).then_inc(abs_ready, 1)

            def sign(src, w):
                act.activation(q_signed[:, :w], src[:, :w], ACT.Sign).then_inc(sign_ready, 1)

            def weights_in(i):
                src, w = (sig, hh)[i % 2], pieces[i][1]
                act.wait_ge(in_wq[i % 2], 16 * (i // 2 + 1))
                if i >= 1:
                    act.wait_ge(wq_ready, i)
                absolute(src, w)
                sign(src, w)

            def weights_high(i):
                act.wait_ge(wq_turned, i + 1)
                _, _, tiles, k = pieces[i]
                b0, b1_ = turn_banks(i)
                if tiles:
                    for t in range(tiles[1]):
                        src = (b0, b1_)[t // 2][:, t % 2 * D:(t % 2 + 1) * D]
                        a = act.activation(wgu_t[:, HIGH, :, (tiles[0] + t) * P:(tiles[0] + t + 1) * P],
                                           src.rearrange("p (k r) -> p k r", k=KD), ACT.Copy)
                else:
                    cols = slice(k * P, (k + 1) * P)
                    act.activation(wdown_t[:, HIGH, :4, cols], b0[:].rearrange("p (f r) -> p f r", r=P), ACT.Copy)
                    act.activation(wdown_t[:, HIGH, 4, cols], b1_[:, :P], ACT.Copy)
                    a = act.activation(wdown_t[:FR, HIGH, 5, cols], b1_[:FR, P:2 * P], ACT.Copy)
                a.then_inc(wq_high, 1)

            def absolute_o(n):
                act.wait_ge(chain, C0 + n * CHAIN + 1)
                absolute(o_s, D)

            def keep_oq(n):
                act.wait_ge(oq_turned, n + 1)
                act.activation(turned[:, :D], turn_a[:, :D], ACT.Copy)
                act.activation(oq_t[:, HIGH].rearrange("p k t -> p (k t)"), turn_a[:, :D], ACT.Copy).then_inc(oq_high, 1)

            def sigmoid(n, i):
                (n0, w), bk = gu_tiles[i], gu_banks[i]
                act.wait_ge(gu_done, 3 * n + i + 1)
                act.activation(sig[:, n0 * 64:(n0 + w) * 64].rearrange("p (j r) -> p j r", r=64),
                               bk[:, :w * P].rearrange("p (j r) -> p j r", r=P)[:, :, :64],
                               ACT.Sigmoid).then_inc(sig_ready, 1)

            def absolute_h(n):
                act.wait_ge(chain, C0 + n * CHAIN + GATED)
                absolute(hh, FF)

            def keep_hq(n, part):
                act.wait_ge(hq_turned, 2 * n + part + 1)
                if part == 0:
                    act.activation(turned[:, :3 * P], turn_a[:, :3 * P], ACT.Copy)
                    act.activation(hq_t[:, HIGH, :3].rearrange("p f t -> p (f t)"), turn_a[:, :3 * P], ACT.Copy)
                else:
                    act.activation(turned[:, 3 * P:5 * P], mm_c[:, :2 * P], ACT.Copy)
                    act.activation(turned[:FR, 5 * P:], mm_c[:FR, 2 * P:3 * P], ACT.Copy)
                    act.activation(hq_t[:, HIGH, 3:5].rearrange("p f t -> p (f t)"), mm_c[:, :2 * P], ACT.Copy)
                    act.activation(hq_t[:FR, HIGH, 5], mm_c[:FR, 2 * P:3 * P], ACT.Copy).then_inc(hq_high, 1)

            def keep_x1(n):
                act.wait_ge(x1_turned, n + 1)
                act.activation(turned[:, :D], turn_a[:, :D], ACT.Copy)
                act.activation(x1_t[:, :, HIGH], turn_a[:, :D].rearrange("p (k t) -> p k t", k=KD), ACT.Copy).then_inc(x1_high, 1)

            def keep_xp(n, g):
                act.wait_ge(xp_done, 3 * n + g + 1)
                act.activation(xp[:, g].rearrange("p (t m b) -> p m b t", t=STEPS, m=KD),
                               (mm_a, mm_b, mm_c)[g][:].rearrange("p (m a b t) -> p m a b t", m=KD, a=2, b=B)[:, :, 0],
                               ACT.Copy, scale=GATE_SCALE).then_inc(xp_half, 1)

            def gate_functions(c, s):
                col, w = s * KD * B, KD * B
                st = c * STEPS + s
                act.wait_ge(g_done, st + 1)
                act.activation(fold0[:, s % 2, 4:4 + 4 * w].rearrange("p (a b) -> p a b", b=4)[:, :, 0:2],
                               gate_g[:, col:col + w].unsqueeze(2).to_broadcast([P, w, 2]),
                               ACT.Tanh, scale=1.0 / GATE_SCALE)
                act.wait_ge(f_done, st + 1)
                act.activation(fold1[:, 4:4 + 4 * w:4], gate_f[:, col:col + w], ACT.Sigmoid,
                               scale=1.0 / GATE_SCALE).then_inc(f_ready, 1)
                act.wait_ge(o_done, st + 1)
                act.activation(so[:], gate_o[:, col:col + w], ACT.Sigmoid, scale=1.0 / GATE_SCALE).then_inc(o_ready, 1)
                act.wait_ge(c_ready, st + 1)
                act.activation(tc[:], fold0[:, (s + 1) % 2, 3:3 + 4 * w:4], ACT.Tanh).then_inc(tc_ready, 1)

            def keep_onehot(m):
                act.wait_ge(oh_turned, m + 1)
                act.activation(oh_tb[:], turn_a[:E, :P], ACT.Copy)
                act.activation(oh_t[:], turn_a[:E, :P], ACT.Copy).then_inc(oht_ready, 1)

            def hidden(m, q, part):
                hb = hid_banks[q][0]
                if part == 0:
                    act.wait_ge(hid_done, m * NQ + q + 1)
                for j in range(2 * part, 2 * part + 2):
                    b0 = q * GRP + j
                    a = act.activation(hid[:, q % 2, j], hb[:, j * P:(j + 1) * P], ACT.Relu, bias=b1_s[:, b0:b0 + 1],
                                       scale=1.0 / GATE_SCALE)
                if part == 1:
                    a.then_inc(hid_ready, 1)

            def hid_highs(m, q):
                act.wait_ge(hid_masked, m * NQ + q + 1)
                act.activation(hid_r[:, q % 2, HIGH], hid[:, q % 2], ACT.Copy).then_inc(hid_high, 1)

            def background(c, s):
                n = c + 1
                if s == 4:
                    absolute_o(n)
                elif s == 5:
                    keep_onehot(c)
                elif s == 6:
                    sign(o_s, D)
                elif s in (8, 9):
                    hidden(c, 0, s - 8)
                elif s == 11:
                    hid_highs(c, 0)
                elif s in (13, 14):
                    hidden(c, 1, s - 13)
                    if s == 14:
                        keep_oq(n)
                elif s == 16:
                    hid_highs(c, 1)
                elif s in (20, 24, 27):
                    sigmoid(n, {20: 0, 24: 1, 27: 2}[s])
                elif s == 29:
                    absolute_h(n)
                elif s == 30:
                    sign(hh, FF)
                elif s in (33, 34):
                    hidden(c, 2, s - 33)
                elif s == 36:
                    hid_highs(c, 2)
                elif s in (41, 42):
                    hidden(c, 3, s - 41)
                    if s == 42:
                        keep_hq(n, 0)
                elif s == 43:
                    keep_hq(n, 1)
                elif s == 45:
                    hid_highs(c, 3)
                elif s == 52:
                    keep_x1(n)
                elif s in (57, 58, 60):
                    keep_xp(n, {57: 0, 58: 1, 60: 2}[s])

            high_stage(0)
            for i in range(NW):
                if i == GUW:
                    act.wait_ge(chain, O0)
                    absolute(o_s, D)
                    sign(o_s, D)
                    weights_high(GUW - 1)
                    keep_oq(0)
                weights_in(i)
                if 1 <= i < GUW:
                    weights_high(i - 1)
                if i == 1:
                    act.wait_ge(setup_v, 6)
                    act.activation(dsq, dvar, ACT.Sqrt).then_inc(setup_act, 1)
                for j in range(2 * i + 1, min(2 * i + 3, NS)):
                    high_stage(j)
            act.wait_ge(in_small, 64)
            act.activation(b2_r[:, HIGH], b2_s[:], ACT.Copy).then_inc(small_high, 1)
            act.activation(router_h[:, HIGH], router_s[:], ACT.Copy, scale=W_SCALE)
            act.activation(router_s[:], router_s[:], ACT.Copy, scale=W_SCALE).then_inc(small_high, 1)
            weights_high(GUW)
            for i in range(len(gu_tiles)):
                sigmoid(0, i)
            weights_high(NW - 1)
            absolute_h(0)
            sign(hh, FF)
            keep_hq(0, 0)
            keep_hq(0, 1)
            keep_x1(0)
            for g in range(3):
                keep_xp(0, g)
            with act.Fori(0, CH) as c:
                for s in range(STEPS):
                    gate_functions(c, s)
                    background(c, s)
            keep_onehot(CH)
            for q in range(NQ):
                hidden(CH, q, 0)
                hidden(CH, q, 1)
                hid_highs(CH, q)

        @block.vector
        def _(v):
            def quantise(k, i, src, dst, w, base):
                nb = w // QB
                mag, half, whole = q_mag[:, :w], q_half[:, :w], q_whole[:, :w]

                def blocks(t):
                    return t.rearrange("p (n q) -> p n q", q=QB)

                v.wait_ge(chain, base + (k - 1 if 5 <= k <= 10 else k))
                if k == 0:
                    v.tensor_reduce(q_amax[:, :nb], blocks(src[:, :w]), AX.X, ALU.max,
                                    apply_absolute_value=True).then_inc(chain, 1)
                elif k == 1:
                    v.tensor_scalar(q_scale[:, :nb], q_amax[:, :nb], 1.0 / 6.0, 1e-12, ALU.mult, ALU.max).then_inc(chain, 1)
                elif k == 2:
                    v.reciprocal(q_inv[:, :nb], q_scale[:, :nb]).then_inc(chain, 1)
                elif k == 3:
                    v.wait_ge(abs_ready, i + 1)
                    v.tensor_tensor(blocks(mag), blocks(mag), q_inv[:, :nb].unsqueeze(2).to_broadcast([P, nb, QB]),
                                    ALU.mult).then_inc(chain, 1)
                elif k == 4:
                    v.tensor_scalar(half, mag, 0.25, None, ALU.is_gt).then_inc(chain, 1)
                elif k == 5:
                    v.tensor_scalar(whole, mag, 5.0, 2.0, ALU.is_gt, ALU.mult).then_inc(chain, 1)
                elif k <= 10:
                    acc = half if k % 2 == 0 else whole
                    mid = (0.75, 3.5, 1.25, 2.5, 1.75)[k - 6]
                    v.scalar_tensor_tensor(acc, mag, mid, acc, ALU.is_gt, ALU.add).then_inc(chain, 1)
                elif k == 11:
                    v.scalar_tensor_tensor(mag, whole, 2.0, half, ALU.mult, ALU.add).then_inc(chain, 1)
                else:
                    v.wait_ge(signed_ready, i + 1)
                    return v.scalar_tensor_tensor(dst[:, :w], mag, 0.5, q_signed[:, :w], ALU.mult, ALU.mult)

            v.memset(zeros[:], 0.0).then_inc(setup_v, 1)
            v.memset(fold1[:], 1.0).then_inc(chain, 1)
            v.memset(fold0[:], 0.0).then_inc(setup_v, 1)
            v.memset(y_s[:], 0.0).then_inc(y_free, 16)
            v.memset(hist[:], 0.0)
            v.memset(ht_h[:], 0.0)
            v.memset(x1_prev[:], 0.0)
            v.wait_ge(chain, 1)
            v.memset(fold1[:, 2::4], 0.0)
            v.wait_ge(in_cond, 16)
            v.tensor_scalar(ys[:], cond_s[:], D ** -0.5, None, ALU.mult).then_inc(setup_v, 1)
            v.tensor_scalar(h16[:, 0, 0], cond_s[:], H_SCALE, None, ALU.mult).then_inc(hi_ready, 1)
            v.wait_ge(setup_v, 3)
            v.tensor_tensor(ys2[:], ys[:], ys[:], ALU.mult).then_inc(setup_v, 1)
            v.tensor_copy(fold0[:, 0, 3:3 + 4 * KD * B:4], cond_s[:].rearrange("p k b -> p (k b)"))
            v.wait_ge(setup_v, 4)
            v.tensor_copy(ys2_b[:, :KD].rearrange("p k (b t) -> p k b t", b=B),
                          ys2[:].unsqueeze(3).to_broadcast([P, KD, B, STEPS])).then_inc(setup_v, 1)
            v.wait_ge(hi_ready, 1)
            v.scalar_tensor_tensor(h16[:, 0, 1], cond_s[:], H_SCALE, h16[:, 0, 0], ALU.mult,
                                   ALU.subtract).then_inc(lo_ready, 1)

            def weights_quantised(i):
                src, w = (sig, hh)[i % 2], pieces[i][1]
                v.wait_ge(in_wq[i % 2], 16 * (i // 2 + 1))
                at, base = place(i)
                for k in range(12):
                    quantise(k, at, src, None, w, base)
                if i >= 2:
                    v.wait_ge(wq_turned, i - 1)
                quantise(12, at, src, (hq, hq_odd)[i % 2], w, base).then_inc(wq_ready, 1)

            def weights_low(i):
                v.wait_ge(wq_high, i + 1)
                _, _, tiles, k = pieces[i]
                b0, b1_ = turn_banks(i)
                if tiles:
                    for t in range(tiles[1]):
                        src = (b0, b1_)[t // 2][:, t % 2 * D:(t % 2 + 1) * D]
                        cols = slice((tiles[0] + t) * P, (tiles[0] + t + 1) * P)
                        op = v.tensor_tensor(wgu_t[:, LOW, :, cols], src.rearrange("p (k r) -> p k r", k=KD),
                                             wgu_t[:, HIGH, :, cols].bitcast(F32), ALU.subtract)
                else:
                    cols = slice(k * P, (k + 1) * P)
                    v.tensor_tensor(wdown_t[:, LOW, :4, cols], b0[:].rearrange("p (f r) -> p f r", r=P),
                                    wdown_t[:, HIGH, :4, cols].bitcast(F32), ALU.subtract)
                    v.tensor_tensor(wdown_t[:, LOW, 4, cols], b1_[:, :P], wdown_t[:, HIGH, 4, cols].bitcast(F32),
                                    ALU.subtract)
                    op = v.tensor_tensor(wdown_t[:FR, LOW, 5, cols], b1_[:FR, P:2 * P],
                                         wdown_t[:FR, HIGH, 5, cols].bitcast(F32), ALU.subtract)
                op.then_inc(wq_split, 1)

            def modulate(n):
                v.wait_ge(in_xt, 16 * (n + 1))
                v.tensor_tensor(xm[:].rearrange("p k (b t) -> p (k b) t", b=B),
                                xt_s[:].rearrange("p k (b t) -> p (k b) t", b=B),
                                ys[:].rearrange("p k b -> p (k b)").unsqueeze(2).to_broadcast([P, KD * B, STEPS]),
                                ALU.mult).then_inc(xm_ready, 1)
                v.wait_ge(xm_ready, n + 1)
                v.tensor_copy(xm_r[:, HIGH], xm[:]).then_inc(xm_high, 1)

            def demodulate(n):
                v.wait_ge(mod_done, n + 1)
                v.tensor_tensor(o_s[:], mm_a[:, :D], demod[:], ALU.mult).then_inc(chain, 1)

            def quantise_o(n, k):
                if n is None:
                    last = quantise(k, GUW, o_s, oq, D, O0)
                else:
                    last = quantise(k, NW + 2 * n, o_s, oq, D, C0 + n * CHAIN + 1)
                if k == 12:
                    last.then_inc(oq_ready, 1)

            def swiglu(n, i):
                k0 = C0 + n * CHAIN + 1 + STEPS_Q
                (n0, w), bk = gu_tiles[i], gu_banks[i]
                f = slice(n0 * 64, (n0 + w) * 64)
                both = bk[:, :w * P].rearrange("p (j r) -> p j r", r=P)
                v.wait_ge(sig_ready, 3 * n + i + 1)
                v.tensor_tensor(gs[:, f].rearrange("p (j r) -> p j r", r=64), both[:, :, :64],
                                sig[:, f].rearrange("p (j r) -> p j r", r=64), ALU.mult).then_inc(chain, 1)
                v.wait_ge(chain, k0 + 2 * i + 1)
                v.tensor_tensor(hh[:, f].rearrange("p (j r) -> p j r", r=64), both[:, :, 64:],
                                gs[:, f].rearrange("p (j r) -> p j r", r=64), ALU.mult).then_inc(chain, 1)

            def quantise_h(n, k):
                last = quantise(k, NW + 2 * n + 1, hh, hq, FF, C0 + n * CHAIN + GATED)
                if k == 12:
                    last.then_inc(hq_ready, 1)

            def residual(n):
                v.wait_ge(in_x, 16 * (n + 1))
                v.wait_ge(down_done, n + 1)
                v.tensor_tensor(x1[:], mm_a[:, :D], x_s[:], ALU.add).then_inc(x1_ready, 1)

            def add_xp(n, g):
                v.wait_ge(xp_half, 3 * n + g + 1)
                both = (mm_a, mm_b, mm_c)[g][:].rearrange("p (m a b t) -> p m a b t", m=KD, a=2, b=B)
                dst = xp[:, g].rearrange("p (t m b) -> p m b t", t=STEPS, m=KD)
                for m in range(KD):
                    op = v.scalar_tensor_tensor(dst[:, m], both[:, m, 1], GATE_SCALE, dst[:, m], ALU.mult, ALU.add)
                op.then_inc(xp_ready, 1)

            def seed(s):
                w = KD * B
                v.tensor_copy(gates[:, :, s * w:(s + SEED) * w], xp[:, :, s * w:(s + SEED) * w]).then_inc(seeded, 1)

            def cell(c, s):
                w = KD * B
                st = c * STEPS + s
                v.wait_ge(f_ready, st + 1)
                v.tensor_tensor_scan(fold0[:, (s + 1) % 2, 0:4 * w], fold0[:, s % 2, 2:2 + 4 * w],
                                     fold1[:, 2:2 + 4 * w], 0.0, ALU.subtract, ALU.mult).then_inc(c_ready, 1)
                if s % SEED == 0 and s + SEED < STEPS:
                    v.wait_ge(o_ready, st + 1)
                    seed(s + SEED)
                elif s == STEPS - 2:
                    v.wait_ge(o_ready, st + 1)
                    v.wait_ge(xp_ready, 3 * (c + 2))
                    seed(0)
                v.wait_ge(tc_ready, st + 1)
                nxt = h16[:, (s + 1) % 2]
                v.scalar_tensor_tensor(nxt[:, 0].rearrange("p k b -> p (k b)"), so[:], H_SCALE, tc[:],
                                       ALU.mult, ALU.mult).then_inc(hi_ready, 1)
                v.scalar_tensor_tensor(hist[:, s].rearrange("p k b -> p (k b)"), so[:], H_SCALE, tc[:],
                                       ALU.mult, ALU.mult).then_inc(h_ready, 1)
                v.wait_ge(h_ready, st + 1)
                v.tensor_tensor(nxt[:, 1], hist[:, s], nxt[:, 0], ALU.subtract).then_inc(lo_ready, 1)

            def states(part, t0, t1):
                for k in range(KD):
                    src = hist[:, t0:t1, k].rearrange("p t b -> p b t")
                    high = ht_h[:, HIGH, k].rearrange("p (b t) -> p b t", b=B)[:, :, t0:t1]
                    if part == HIGH:
                        op = v.tensor_copy(high, src)
                    else:
                        low = ht_h[:, LOW, k].rearrange("p (b t) -> p b t", b=B)[:, :, t0:t1]
                        op = v.tensor_tensor(low, src, high, ALU.subtract)
                op.then_inc((ht_high, ht_split)[part], 1)

            def states_late(m):
                states(HIGH, 3 * STEPS // 4, STEPS)
                v.wait_ge(ht_high, 2 * m + 1)
                states(LOW, 3 * STEPS // 4, STEPS)

            def route(m, k):
                k0 = m * MOE_CHAIN
                if k == 0:
                    v.wait_ge(logits_done, m + 1)
                    v.scalar_tensor_tensor(logits[:], turn_a[:, :E], 1.0 / GATE_SCALE, rb_s[:], ALU.mult,
                                           ALU.add).then_inc(moe_chain, 1)
                    v.wait_ge(moe_chain, k0 + 1)
                    v.tensor_reduce(top[:], logits[:], AX.X, ALU.max).then_inc(moe_chain, 1)
                    v.wait_ge(moe_chain, k0 + 2)
                    v.scalar_tensor_tensor(cand[:], logits[:], top[:, 0:1], iota_m[:], ALU.is_equal,
                                           ALU.mult).then_inc(moe_chain, 1)
                else:
                    v.wait_ge(moe_chain, k0 + 3)
                    v.tensor_reduce(first[:], cand[:], AX.X, ALU.min).then_inc(moe_chain, 1)
                    v.wait_ge(moe_chain, k0 + 4)
                    v.tensor_scalar(onehot[:], iota_m[:], first[:, 0:1], None, ALU.is_equal).then_inc(top_ready, 1)

            def mask(m, q):
                v.wait_ge(hid_ready, m * NQ + q + 1)
                rows = hid[:, q % 2].rearrange("p j t -> p (j t)")
                v.tensor_tensor(rows, hid_banks[q][1][:], rows, ALU.mult).then_inc(hid_masked, 1)

            def finish(m):
                v.wait_ge(y_done, m + 1)
                v.wait_ge(y_free, 16 * (m + 1))
                v.scalar_tensor_tensor(y_s[:], turn_b[:, :D], 0.0, x1_old[:], ALU.max, ALU.add).then_inc(y_ready, 1)

            steps_o = {4: (0, 1, 2), 5: (3, 4), 6: (5, 6, 7), 7: (8, 9), 8: (10, 11), 9: (12,)}
            steps_h = {29: (0,), 30: (1, 2), 31: (3,), 32: (4, 5), 33: (6,), 34: (7,), 36: (8,), 37: (9,), 38: (10,),
                       39: (11,), 40: (12,)}

            def background(c, s):
                n = c + 1
                for k in steps_o.get(s, ()):
                    quantise_o(n, k)
                for k in steps_h.get(s, ()):
                    quantise_h(n, k)
                if s == 0:
                    states_late(c)
                elif s in (2, 3):
                    route(c, s - 2)
                    if s == 3:
                        demodulate(n)
                elif s in (10, 15, 35, 43):
                    mask(c, {10: 0, 15: 1, 35: 2, 43: 3}[s])
                elif s in (21, 25, 28):
                    swiglu(n, {21: 0, 25: 1, 28: 2}[s])
                elif s == 48:
                    states(HIGH, 0, 3 * STEPS // 4)
                elif s == 49:
                    v.wait_ge(ht_high, 2 * c + 2)
                    states(LOW, 0, 3 * STEPS // 4)
                elif s == 46:
                    v.tensor_copy(x1_old[:], x1_prev[:])
                elif s == 47:
                    v.tensor_copy(x1_prev[:], x1[:])
                elif s == 50:
                    residual(n)
                elif s == 55:
                    modulate(c + 2)
                elif s in (58, 59, 61):
                    add_xp(n, {58: 0, 59: 1, 61: 2}[s])
                elif s == 63:
                    finish(c)

            weights_quantised(0)
            v.wait_ge(setup_pe, 4)
            v.tensor_scalar(dvar, turn_b[:, :D], 1e-8, None, ALU.add).then_inc(setup_v, 1)
            weights_quantised(1)
            weights_low(0)
            modulate(0)
            weights_quantised(2)
            weights_low(1)
            weights_quantised(3)
            weights_low(2)
            D0 = 1 + GUW * STEPS_Q
            v.wait_ge(setup_act, 1)
            v.reciprocal(dinv, dsq).then_inc(chain, 1)
            v.wait_ge(chain, D0 + 1)
            v.tensor_tensor(dtmp, dinv, dinv, ALU.mult).then_inc(chain, 1)
            v.wait_ge(chain, D0 + 2)
            v.tensor_tensor(dtmp, dtmp, dvar, ALU.mult).then_inc(chain, 1)
            v.wait_ge(chain, D0 + 3)
            v.tensor_scalar(dtmp, dtmp, -0.5, 1.5, ALU.mult, ALU.add).then_inc(chain, 1)
            v.wait_ge(chain, D0 + 4)
            v.tensor_tensor(demod[:], dinv, dtmp, ALU.mult).then_inc(chain, 1)
            v.wait_ge(chain, D0 + 5)
            demodulate(0)
            for k in range(13):
                quantise_o(None, k)
            weights_low(3)
            weights_quantised(4)
            weights_quantised(5)
            weights_low(4)
            for i in range(len(gu_tiles)):
                swiglu(0, i)
            weights_low(5)
            for k in range(13):
                quantise_h(0, k)
            residual(0)
            modulate(1)
            for g in range(3):
                add_xp(0, g)
            v.wait_ge(xp_ready, 3)
            seed(0)
            with v.Fori(0, CH) as c:
                for s in range(STEPS):
                    cell(c, s)
                    background(c, s)
            states_late(CH)
            v.wait_ge(y_ready, CH)
            v.tensor_copy(x1_old[:], x1_prev[:])
            route(CH, 0)
            route(CH, 1)
            for q in range(NQ):
                mask(CH, q)
            finish(CH)


def kernel(**inputs):
    import numpy as np
    import concourse.bacc as bacc
    from concourse.bass_utils import run_bass_kernel_spmd

    a = {k: np.ascontiguousarray(v) for k, v in inputs.items()}
    x = a["x"]
    B, S, D = x.shape
    CH, T = S * B // P, P // B
    KD = D // P
    xc = x.reshape(B, CH, T, D).transpose(1, 0, 2, 3).reshape(CH, P, D)
    FF = a["L0_ffn_w_gate"].shape[0]
    gu = np.concatenate([a["L0_ffn_w_gate"].reshape(FF // 64, 64, D), a["L0_ffn_w_up"].reshape(FF // 64, 64, D)], axis=1)
    E, _, H = a["L1_ffn_weights1"].shape

    def halves(w):
        return w.reshape(KD, P, -1).transpose(1, 0, 2)

    laid = {
        "x": xc,
        "xt": xc.transpose(0, 2, 1).reshape(CH, KD, P, P).transpose(0, 2, 1, 3),
        "condt": halves(a["cond_1024"].T),
        "w_mod": halves(a["L0_cond_weight"]),
        "w_gu": gu.transpose(1, 0, 2),
        "w_down": halves(a["L0_ffn_w_down"]),
        "wk": halves(a["L1_cond_Wk"]),
        "wr": halves(a["L1_cond_Wr"]),
        "router": halves(a["L1_ffn_router_w"].T),
        "router_b": np.broadcast_to(a["L1_ffn_router_b"], (P, E)),
        "w1": halves(a["L1_ffn_weights1"].transpose(1, 0, 2).reshape(D, E * H)),
        "b1": a["L1_ffn_bias1"].reshape(E * H // P, P).T,
        "w2": a["L1_ffn_weights2"].reshape(E * H // P, P, D).transpose(1, 0, 2),
        "b2": a["L1_ffn_bias2"],
    }
    laid = {k: np.ascontiguousarray(v) for k, v in laid.items()}
    nc = bacc.Bacc("TRN2", target_bir_lowering=False, num_devices=1, dynamic_dma_scratch_size=1024)
    args = [nc.dram_tensor(f"in_{k}", v.shape, mybir.dt.from_np(v.dtype), kind="ExternalInput").ap() for k, v in laid.items()]
    args.append(nc.dram_tensor("out", (CH, P, D), F32, kind="ExternalOutput").ap())
    build(nc, *args)
    r = run_bass_kernel_spmd(nc, [{f"in_{k}": v for k, v in laid.items()}], core_ids=[0])
    got = r.results[0]["out"]
    return got.reshape(CH, B, T, D).transpose(1, 0, 2, 3).reshape(B, S, D)
```
